# Optimizing a Trainium2 kernel written in Bass

```python
import numpy as np
import jax
import jax.numpy as jnp

def _softmax(x, axis=-1):
    return jax.nn.softmax(x, axis=axis)

def _gelu(x):
    return jax.nn.gelu(x, approximate=True)

def _silu(x):
    return jax.nn.silu(x)

def _sigmoid(x):
    return jax.nn.sigmoid(x)

def _layernorm(x, axis=-1, eps=1e-05):
    m = jnp.mean(x, axis=axis, keepdims=True)
    v = jnp.var(x, axis=axis, keepdims=True)
    return (x - m) / jnp.sqrt(v + eps)

def _scatter_add(tgt, idx, src, axis=0):
    return tgt.at[idx].add(src)

def _segment_sum(src, seg, n):
    return jax.ops.segment_sum(src, seg, n)
kernel_name = 'mk_seq_preln_d1_jaxref_r4_ee3695'

def setup_inputs(seed: int=0):
    np.random.seed(seed)
    _w = jnp.asarray

    def _L0_attn_setup():
        import jax, jax.numpy as jnp
        import numpy as np
        import math
        D_MODEL, N_HEADS, D_K, D_C, D_HR = (256, 8, 128, 32, 32)
        B, S = (4, 512)
        key = jax.random.key(seed)
        ks = jax.random.split(key, 17)

        def lin(k, fan_in, fan_out):
            lim = 1.0 / math.sqrt(fan_in)
            kw, kb = jax.random.split(k)
            W = jax.random.uniform(kw, (fan_in, fan_out), jnp.float32, -lim, lim)
            b = jax.random.uniform(kb, (fan_out,), jnp.float32, -lim, lim)
            return (W, b)
        W_DQ, b_DQ = lin(ks[0], D_MODEL, D_C)
        W_UQ, b_UQ = lin(ks[1], D_C, N_HEADS * D_K)
        W_DKV, b_DKV = lin(ks[2], D_MODEL, D_C)
        W_UK, b_UK = lin(ks[3], D_C, N_HEADS * D_K)
        W_UV, b_UV = lin(ks[4], D_C, N_HEADS * D_K)
        W_QR, b_QR = lin(ks[5], D_C, N_HEADS * D_HR)
        W_KR, b_KR = lin(ks[6], D_MODEL, D_HR)
        W_O, b_O = lin(ks[7], N_HEADS * D_K, D_MODEL)
        h_t = jax.random.normal(ks[8], (B, S, D_MODEL), jnp.float32)
        return {'h_t': h_t, 'W_DQ': W_DQ, 'b_DQ': b_DQ, 'W_UQ': W_UQ, 'b_UQ': b_UQ, 'W_DKV': W_DKV, 'b_DKV': b_DKV, 'W_UK': W_UK, 'b_UK': b_UK, 'W_UV': W_UV, 'b_UV': b_UV, 'W_QR': W_QR, 'b_QR': b_QR, 'W_KR': W_KR, 'b_KR': b_KR, 'W_O': W_O, 'b_O': b_O}
    _L0_attn_in = _L0_attn_setup()

    def _L0_ffn_setup():
        import jax, jax.numpy as jnp
        import numpy as np
        EPS = 1e-05

        def _quantize(W):
            gamma = jnp.mean(jnp.abs(W))
            return jnp.clip(jnp.round(W / (gamma + EPS)), -1.0, 1.0)
        key = jax.random.key(seed)
        k_x, k_w1, k_b1, k_w2, k_b2 = jax.random.split(key, 5)
        n_embd = 256
        d_ff = 4 * n_embd
        B, S = (4, 1024)
        bound1 = 1.0 / np.sqrt(n_embd)
        bound2 = 1.0 / np.sqrt(d_ff)
        x = jax.random.normal(k_x, (B, S, n_embd), dtype=jnp.float32)
        W1 = jax.random.uniform(k_w1, (d_ff, n_embd), jnp.float32, -bound1, bound1)
        b1 = jax.random.uniform(k_b1, (d_ff,), jnp.float32, -bound1, bound1)
        W2 = jax.random.uniform(k_w2, (n_embd, d_ff), jnp.float32, -bound2, bound2)
        b2 = jax.random.uniform(k_b2, (n_embd,), jnp.float32, -bound2, bound2)
        return {'x': x, 'W1': W1, 'b1': b1, 'W2': W2, 'b2': b2}
    _L0_ffn_in = _L0_ffn_setup()
    _d = {'L0_attn_h_t': _L0_attn_in['h_t'], 'L0_attn_W_DQ': _L0_attn_in['W_DQ'], 'L0_attn_b_DQ': _L0_attn_in['b_DQ'], 'L0_attn_W_UQ': _L0_attn_in['W_UQ'], 'L0_attn_b_UQ': _L0_attn_in['b_UQ'], 'L0_attn_W_DKV': _L0_attn_in['W_DKV'], 'L0_attn_b_DKV': _L0_attn_in['b_DKV'], 'L0_attn_W_UK': _L0_attn_in['W_UK'], 'L0_attn_b_UK': _L0_attn_in['b_UK'], 'L0_attn_W_UV': _L0_attn_in['W_UV'], 'L0_attn_b_UV': _L0_attn_in['b_UV'], 'L0_attn_W_QR': _L0_attn_in['W_QR'], 'L0_attn_b_QR': _L0_attn_in['b_QR'], 'L0_attn_W_KR': _L0_attn_in['W_KR'], 'L0_attn_b_KR': _L0_attn_in['b_KR'], 'L0_attn_W_O': _L0_attn_in['W_O'], 'L0_attn_b_O': _L0_attn_in['b_O'], 'L0_ffn_W1': _L0_ffn_in['W1'], 'L0_ffn_b1': _L0_ffn_in['b1'], 'L0_ffn_W2': _L0_ffn_in['W2'], 'L0_ffn_b2': _L0_ffn_in['b2']}
    _x0 = _d['L0_attn_h_t']
    _d['L0_attn_h_t'] = jax.random.normal(jax.random.fold_in(jax.random.key(seed), 1), (16, 512, 256), dtype=_x0.dtype)
    del _x0
    return _d

def reference(L0_attn_h_t, L0_attn_W_DQ, L0_attn_b_DQ, L0_attn_W_UQ, L0_attn_b_UQ, L0_attn_W_DKV, L0_attn_b_DKV, L0_attn_W_UK, L0_attn_b_UK, L0_attn_W_UV, L0_attn_b_UV, L0_attn_W_QR, L0_attn_b_QR, L0_attn_W_KR, L0_attn_b_KR, L0_attn_W_O, L0_attn_b_O, L0_ffn_W1, L0_ffn_b1, L0_ffn_W2, L0_ffn_b2):

    def _L0_attn_ref(h_t, W_DQ, b_DQ, W_UQ, b_UQ, W_DKV, b_DKV, W_UK, b_UK, W_UV, b_UV, W_QR, b_QR, W_KR, b_KR, W_O, b_O):
        import jax, jax.numpy as jnp
        import numpy as np
        import math
        D_MODEL, N_HEADS, D_K, D_C, D_HR = (256, 8, 128, 32, 32)
        B, S = (4, 512)
        b, s, _ = h_t.shape
        c_q = h_t @ W_DQ + b_DQ
        c_kv = h_t @ W_DKV + b_DKV
        q_c = (c_q @ W_UQ + b_UQ).reshape(b, s, N_HEADS, D_K).transpose(0, 2, 1, 3)
        k_c = (c_kv @ W_UK + b_UK).reshape(b, s, N_HEADS, D_K).transpose(0, 2, 1, 3)
        v_c = (c_kv @ W_UV + b_UV).reshape(b, s, N_HEADS, D_K).transpose(0, 2, 1, 3)
        q_r = (c_q @ W_QR + b_QR).reshape(b, s, N_HEADS, D_HR).transpose(0, 2, 1, 3)
        k_r = (h_t @ W_KR + b_KR)[:, None, :, :]
        k_r = jnp.broadcast_to(k_r, (b, N_HEADS, s, D_HR))
        q = jnp.concatenate([q_c, q_r], axis=-1)
        k = jnp.concatenate([k_c, k_r], axis=-1)
        scale = 1.0 / math.sqrt(D_K + D_HR)
        scores = jnp.einsum('bhsd,bhtd->bhst', q, k) * scale
        attn = jax.nn.softmax(scores, axis=-1)
        o = jnp.einsum('bhst,bhtd->bhsd', attn, v_c)
        o = o.transpose(0, 2, 1, 3).reshape(b, s, N_HEADS * D_K)
        return o @ W_O + b_O

    def _L0_ffn_ref(x, W1, b1, W2, b2):
        import jax, jax.numpy as jnp
        import numpy as np
        EPS = 1e-05

        def _quantize(W):
            gamma = jnp.mean(jnp.abs(W))
            return jnp.clip(jnp.round(W / (gamma + EPS)), -1.0, 1.0)
        Wq1 = _quantize(W1)
        Wq2 = _quantize(W2)
        h = jax.nn.relu(jnp.einsum('bsd,fd->bsf', x, Wq1) + b1)
        out = jnp.einsum('bsf,df->bsd', h, Wq2) + b2
        return out
    x = L0_attn_h_t
    x = x + _L0_attn_ref(_layernorm(x, axis=-1), L0_attn_W_DQ, L0_attn_b_DQ, L0_attn_W_UQ, L0_attn_b_UQ, L0_attn_W_DKV, L0_attn_b_DKV, L0_attn_W_UK, L0_attn_b_UK, L0_attn_W_UV, L0_attn_b_UV, L0_attn_W_QR, L0_attn_b_QR, L0_attn_W_KR, L0_attn_b_KR, L0_attn_W_O, L0_attn_b_O)
    x = x + _L0_ffn_ref(_layernorm(x, axis=-1), L0_ffn_W1, L0_ffn_b1, L0_ffn_W2, L0_ffn_b2)
    return x

_drawn_inputs = setup_inputs


def setup_inputs(seed=0):
    import zlib

    import numpy as np

    out = dict(_drawn_inputs(seed))
    spreads = {}
    factors = {'L0_attn_W_DQ': 8.0,
     'L0_attn_b_DQ': 8.0,
     'L0_attn_W_UQ': 8.0,
     'L0_attn_b_UQ': 8.0,
     'L0_attn_W_DKV': 6.816,
     'L0_attn_b_DKV': 5.797,
     'L0_attn_W_UK': 8.0,
     'L0_attn_b_UK': 64.0,
     'L0_attn_W_UV': 4.403,
     'L0_attn_W_QR': 8.0,
     'L0_attn_b_QR': 8.0,
     'L0_attn_W_KR': 8.0,
     'L0_attn_b_KR': 64.0,
     'L0_attn_b_O': 20.044,
     'L0_ffn_b1': 21.624,
     'L0_ffn_b2': 64.0,
     'L0_attn_b_UV': 6.575}
    for name, (base, spread) in spreads.items():
        noise = np.random.default_rng([zlib.crc32(name.encode()), seed]).standard_normal(out[name].shape)
        drawn = base * np.exp(spread * noise) if base else spread * noise
        out[name] = jnp.asarray(drawn.astype(out[name].dtype))
    for name, factor in factors.items():
        out[name] = (out[name] * factor).astype(out[name].dtype)
    return out
```

```python
from contextlib import ExitStack

import concourse.bass as bass
from concourse import mybir

F32 = mybir.dt.float32
F32R = mybir.dt.float32r
ALU = mybir.AluOpType
ACT = mybir.ActivationFunctionType
AX = mybir.AxisListType

P = 128
SLOTS, SEGS = 8, 4

TASKS_A = {(0, 0): "X0", (0, 1): "X1", (0, 2): "K", (0, 3): "C", (1, 1): "Q0", (1, 3): "S", (2, 1): "Q1",
           (2, 3): "R1", (3, 1): "Q2", (4, 1): "Q3", (5, 1): "Q4", (5, 3): "V", (6, 1): "Q5", (6, 3): "R0",
           (7, 1): "Q6", (7, 3): "Q7"}
TASKS_F = {(0, 0): "H0", (0, 2): "H1", (1, 0): "H2", (1, 2): "H3", (2, 0): "H4", (2, 2): "H5", (3, 0): "H6",
           (3, 2): "H7", (4, 0): "O0", (4, 2): "Y0", (5, 0): "O1", (5, 2): "Y1", (6, 1): "T0", (6, 2): "Y2",
           (7, 1): "T1", (7, 2): "Y3"}


class Step:

    def __init__(self, s, nb, parity=None):
        self.s, self.full = s, parity is not None
        self.par = parity if self.full else s % 2
        live = lambda b: self.full or 0 <= b < nb
        self.ln, self.qk, self.sm, self.out, self.ffn = (live(s + d) for d in ((2, 1, 0, -1, -2)))

    def has_a(self, task):
        return self.sm if task == "R1" else self.qk

    def has_f(self, task):
        return self.ffn if task[0] in "HY" else self.out


def layer_kernel(nc, x, W_DQ, b_DQ, W_UQ, b_UQ, W_DKV, b_DKV, W_UK, b_UK, W_UV, b_UV, W_QR, b_QR, W_KR, b_KR,
                 W_O, b_O, W1, b1, W2, b2, out):
    NB, S, D = x.shape
    DC = W_DQ.shape[1]
    DR = W_KR.shape[1]
    H = W_QR.shape[1] // DR
    DK = W_UQ.shape[1] // H
    F = W1.shape[0]
    KD = D // P
    NF = F // P
    NT = S // P
    W = DC + DR
    G = 4
    NG = H // G
    KQ = 3 * DC + 2
    SCALE = float(DK + DR) ** -0.5
    MAGIC = 1.5 * 2.0 ** 23
    EPS = 1e-5
    assert (S, D, DC, DR, DK, H) == (512, 256, 32, 32, 128, SLOTS) and NT == SEGS and F == 1024 and NB % 2 == 0

    ctx = ExitStack()
    with ctx:
        def sb(name, shape, dt=F32):
            return ctx.enter_context(nc.sbuf_tensor(name, shape, dt))

        def sem(name):
            return ctx.enter_context(nc.semaphore(name))

        bank = [ctx.enter_context(nc.psum_tensor(n, [P, 512], F32))
                for n in ("bST0", "bST1", "bMX0", "bMX1", "bU", "bL", "bGA", "bGF")]
        ST, MX, U, L, GA, GF = bank[0:2], bank[2:4], bank[4], bank[5], bank[6], bank[7]

        ident = sb("ident", [P, P])
        identr = sb("identr", [P, P], F32R)
        ones32 = sb("ones32", [P, 32])
        neghalf = sb("neghalf", [P, NT])
        headmask = sb("headmask", [P, G])
        wk = sb("wk", [P, KD, P])
        wc = sb("wc", [P, KD, KQ])
        bk = sb("bk", [P, 1])
        bc = sb("bc", [P, 1])
        AQ = sb("AQ", [KQ, H, 2, W], F32R)
        AC = sb("AC", [KQ, H], F32R)
        M = sb("M", [P, NG, D])
        battn = sb("battn", [P, D])
        b2row = sb("b2row", [P, D])
        b1col = sb("b1col", [P, NF])
        w1T = sb("w1T", [P, KD, F], F32R)
        w2T = sb("w2T", [P, NF, D], F32R)
        xln = sb("xln", [P, NT, D])
        xT = sb("xT", [P, KD, S])
        yln = xT[:, :, :].rearrange("p k s -> p (k s)").rearrange("p (t d) -> p t d", t=NT)
        kf = sb("kf", [P, S])
        cq = sb("cq", [P, S], F32R)
        KA = [sb(f"KA{i}", [P, S], F32R) for i in range(2)]
        KB = [sb(f"KB{i}", [P, S], F32R) for i in range(2)]
        V = [sb(f"V{i}", [P, NT, DC]) for i in range(2)]
        QA = sb("QA", [P, H, S], F32R)
        QB = sb("QB", [W + G, H, S], F32R)
        rowmax = sb("rowmax", [P, H, NT])
        const = [sb(f"const{i}", [P, NT, H]) for i in range(2)]
        mfull = sb("mfull", [P, G, NT])
        shift = sb("shift", [P, NT, W + G], F32R)
        E = sb("E", [P, H, NT, S])
        esum = sb("esum", [P, G, S])
        un = sb("un", [P, NG, S])
        x2 = [sb(f"x2_{i}", [P, NT, D]) for i in range(2)]
        stats = sb("stats", [P, NT, 6])
        mv = sb("mv", [P, 2, NT, 2])
        carrier = sb("carrier", [1, 2])
        vareps = sb("vareps", [P, 2, NT])
        rstd = sb("rstd", [P, 2, NT])
        yh = sb("yh", [P, KD, S], F32R)
        yl = sb("yl", [P, KD, S], F32R)
        hh = sb("hh", [P, NF, S], F32R)
        hl = sb("hl", [P, NF, S], F32R)
        ob = sb("ob", [P, 2, D])
        hf = ob[:, :, :].rearrange("p a d -> p (a d)")
        cf = un[0:KQ, 1, :]

        Ef = E[:, :, :, :].rearrange("p h t s -> p (h t s)")
        w1n = Ef[:, 0:2048].rearrange("p (n d) -> p n d", n=NF)
        w2n = Ef[:, 2048:4096].rearrange("p (n f) -> p n f", n=KD)
        wo = Ef[:, 4096:6144].rearrange("p (h n) -> p h n", h=H)
        wuq = Ef[0:DC, 6144:7168]
        wuk = Ef[0:DC, 7168:8192]
        wuv = Ef[0:DC, 8192:9216]
        LQ = Ef[:, 9216:9216 + H * KQ].rearrange("p (h c) -> p h c", h=H)
        RK = Ef[:, 10240:10240 + H * (DC + 1)].rearrange("p (h c) -> p h c", h=H)
        uvT = Ef[:, 10624:10880].rearrange("p (h c) -> p h c", h=H)
        buvb = Ef[:, 11008:12032].rearrange("p (h c) -> p h c", h=H)
        AF = Ef[0:KQ, 12032:12032 + H * (W + 1)].rearrange("p (h c) -> p h c", h=H)
        alr = Ef[0:KQ, 12608:12608 + H * (W + 1)].rearrange("p (h c) -> p h c", h=H)
        colb = Ef[:, 13200:13200 + 3 * H].rearrange("p (k h) -> p k h", k=3)
        ones128 = Ef[:, 13312:13440]
        bot = Ef[:, 13440:13696]
        wabs = Ef[:, 13824:15872]
        gsum = Ef[:, 15900:15902]
        gcol = Ef[:, 15902:15904]
        grec = Ef[:, 15904:15906]
        w_at = sem("w_at")
        w_ff = sem("w_ff")
        memz = sem("memz")
        cst = sem("cst")
        su_pe = sem("su_pe")
        su_dve = sem("su_dve")
        su_act = sem("su_act")
        row_sent = sem("row_sent")
        x_in = sem("x_in")
        xln_done = sem("xln_done")
        ga_full = sem("ga_full")
        ga_free = sem("ga_free")
        gf_full = sem("gf_full")
        gf_free = sem("gf_free")
        k_done = sem("k_done")
        c_done = sem("c_done")
        qh_done = sem("qh_done")
        mx_full = sem("mx_full")
        mx_done = sem("mx_done")
        mf_done = sem("mf_done")
        sh_done = sem("sh_done")
        st_full = sem("st_full")
        e_done = sem("e_done")
        es_done = sem("es_done")
        pv_full = sem("pv_full")
        l_full = sem("l_full")
        rec_done = sem("rec_done")
        un_done = sem("un_done")
        xr_in = sem("xr_in")
        xb_done = sem("xb_done")
        st_done = sem("st_done")
        st2_done = sem("st2_done")
        mv_done = sem("mv_done")
        mv2_done = sem("mv2_done")
        ve_done = sem("ve_done")
        ve2_done = sem("ve2_done")
        rs_done = sem("rs_done")
        rs2_done = sem("rs2_done")
        yln_done = sem("yln_done")
        x2b_done = sem("x2b_done")
        yh_done = sem("yh_done")
        hh_done = sem("hh_done")
        hl_done = sem("hl_done")
        o_sent = [sem(f"o_sent{i}") for i in range(2)]

        def wait(eng, s, value):
            if isinstance(value, int) and value <= 0:
                return
            eng.wait_ge(s, value)

        N_AT = 31

        def a_index(st, task):
            mine = [t for t in TASKS_A.values() if st.has_a(t)].index(task)
            return mine if not st.full and st.s == -1 else st.s * len(TASKS_A) + (len(TASKS_A) - 1) + mine

        def f_index(st, task):
            mine = [t for t in TASKS_F.values() if st.has_f(t)].index(task)
            return mine if not st.full and st.s == 1 else (st.s - 2) * len(TASKS_F) + 4 + mine

        def before(st):
            return Step(st.s - 1, NB, 1 - st.par) if st.full else Step(st.s - 1, NB)

        def f_after_prev(st, task):
            if st.full:
                mine = list(TASKS_F.values()).index(task)
                return (st.s - 3) * len(TASKS_F) + 4 + mine + 1
            p = Step(st.s - 1, NB)
            return f_index(p, task) + 1 if p.has_f(task) else 0

        def steps(eng, body):
            for s in range(-2, 2):
                body(Step(s, NB))
            with eng.Fori(1, NB // 2 - 1) as pair:
                body(Step(pair * 2, NB, 0))
                body(Step(pair * 2 + 1, NB, 1))
            for s in range(NB - 2, NB + 2):
                body(Step(s, NB))

        block = ctx.enter_context(nc.Block())

        @block.sync
        def _(sp):
            def at(dst, src):
                with nc.allow_non_contiguous_dma(reason="short bias columns, once"):
                    sp.dma_start(dst, src).then_inc(w_at, 16)
            sp.wait_ge(memz, 2)
            sp.dma_start(xln[:, :, :], x[0].rearrange("(t p) d -> p t d", p=P)).then_inc(x_in, 16)
            at(wuq, W_UQ)
            at(wuk, W_UK)
            at(wuv, W_UV)
            for j in range(2):
                at(wk[:, :, j * W:j * W + DC], W_DKV.rearrange("(k p) c -> p k c", p=P))
                at(wk[:, :, j * W + DC:(j + 1) * W], W_KR.rearrange("(k p) c -> p k c", p=P))
                at(bk[j * W:j * W + DC, :], b_DKV.rearrange("(c a) -> c a", a=1))
                at(bk[j * W + DC:(j + 1) * W, :], b_KR.rearrange("(c a) -> c a", a=1))
            for j in range(3):
                at(wc[:, :, j * DC:(j + 1) * DC], W_DQ.rearrange("(k p) c -> p k c", p=P))
                at(bc[j * DC:(j + 1) * DC, :], b_DQ.rearrange("(c a) -> c a", a=1))
                at(AF[j * DC:(j + 1) * DC, :, DC:W], W_QR.rearrange("c (h r) -> c h r", h=H))
            for j in range(2):
                at(AF[3 * DC + j:3 * DC + j + 1, :, DC:W], b_QR.rearrange("(a h r) -> a h r", a=1, h=H))
            for j, b in enumerate((b_UQ, b_UK, b_UV)):
                at(colb[:, j, :], b.rearrange("(h p) -> p h", p=P))
            at(wo, W_O.rearrange("(h p) n -> p h n", p=P))
            at(bot, b_O.rearrange("(a n) -> a n", a=1).broadcast_to([P, D]))
            at(w1n, W1.rearrange("(n p) d -> p n d", p=P))
            at(w2n, W2.rearrange("(n p) f -> p n f", p=P))
            at(b1col[:, :], b1.rearrange("(n p) -> p n", p=P))
            at(b2row[:, :], b2.rearrange("(a n) -> a n", a=1).broadcast_to([P, D]))
            sp.wait_ge(su_dve, 9)
            sp.dma_start(AQ[KQ - 1:KQ, :, 0, :].bitcast(F32), alr[KQ - 1:KQ, :, 0:W]).then_inc(row_sent, 16)
            with nc.allow_non_contiguous_dma(reason="eight numbers"):
                sp.dma_start(AC[KQ - 1:KQ, :].bitcast(F32), alr[KQ - 1:KQ, :, W]).then_inc(row_sent, 16)

            def step(st):
                s = st.s
                if st.out:
                    wait(sp, gf_free, f_after_prev(st, "Y3"))
                    b = s - 1
                    sp.dma_start(x2[1 - st.par][:, :, :],
                                 x[bass.ds(b, 1)].rearrange("a (t p) d -> p (a t) d", p=P)).then_inc(xr_in, 16)
                if st.ln and not (not st.full and s == -2):
                    wait(sp, ga_full, a_index(st, "X1") + 1)
                    sp.dma_start(xln[:, :, :],
                                 x[bass.ds(s + 2, 1)].rearrange("a (t p) d -> p (a t) d", p=P)).then_inc(x_in, 16)
                if st.ffn:
                    for t in range(NT):
                        sp.wait_ge(gf_free, f_index(st, f"Y{t}") + 1)
                        sp.dma_start(out[bass.ds(s - 2, 1), t * P:(t + 1) * P, :].rearrange("a p d -> p (a d)"),
                                     ob[:, t % 2, :]).then_inc(o_sent[t % 2], 16)
            steps(sp, step)
            for i in range(2):
                sp.wait_ge(o_sent[i], 8 * NB * NT + 16)

        @block.gpsimd
        def _(pool):
            g = nc.gpsimd
            g.memset(wc[:, :, :], 0.0).then_inc(memz, 1)
            g.memset(bc[:, :], 0.0).then_inc(memz, 1)
            g.memset(ident[:, :], 0.0).then_inc(cst, 1)
            g.memset(headmask[:, :], 0.0).then_inc(cst, 1)
            pool.wait_ge(cst, 2)
            g.affine_select(out=ident[:, :], in_=ident[:, :], compare_op=ALU.not_equal, fill=1.0, base=0,
                            pattern=[[-1, P]], channel_multiplier=1).then_inc(cst, 1)
            g.affine_select(out=headmask[:, :], in_=headmask[:, :], compare_op=ALU.not_equal, fill=1.0, base=-W,
                            pattern=[[-1, G]], channel_multiplier=1).then_inc(cst, 1)
            g.memset(ones32[:, :], 1.0).then_inc(o_sent[0], 16)
            g.memset(neghalf[:, :], -0.5).then_inc(o_sent[1], 16)
            g.memset(ones128, 1.0).then_inc(cst, 1)
            g.memset(shift[:, :, :].bitcast(F32), 0.0).then_inc(cst, 1)

            def shift_group(b, par, gr, prev_full):
                pool.wait_ge(mx_done, b * H * NT + (gr + 1) * G * NT)
                c = const[par][:, :, gr * G:(gr + 1) * G].rearrange("p t h -> p h t")
                g.tensor_tensor(mfull[:, :, :], rowmax[:, gr * G:(gr + 1) * G, :], c, ALU.add).then_inc(mf_done, 1)
                pool.wait_ge(mf_done, b * NG + gr + 1)
                wait(pool, ga_full, prev_full)
                g.tensor_tensor(shift[:, :, W:W + G].rearrange("p t h -> p h t"), c, mfull[:, :, :],
                                ALU.subtract).then_inc(sh_done, 1)

            def step(st):
                s = st.s
                for h in range(SLOTS):
                    if st.out and h == 0:
                        pool.wait_ge(xr_in, s * 16)
                        g.tensor_tensor(x2[1 - st.par][:, :, :], x2[1 - st.par][:, :, :],
                                        battn[:, None, :].broadcast_to([P, NT, D]), ALU.add).then_inc(xb_done, 1)
                    for t in range(SEGS):
                        if st.sm and h == 2 and t == 2:
                            shift_group(s, st.par, 1, a_index(before(st), "R0") + 1)
                        if st.qk and h == 6 and t == 2:
                            wait(pool, ga_free, a_index(st, "S") + 1)
                            shift_group(s + 1, 1 - st.par, 0, a_index(st, "R1") + 1 if st.sm else 0)
                        if st.ln and h == 4 and t == 2:
                            pool.wait_ge(ve_done, s + 3)
                            g.tensor_tensor(rstd[:, 0, :], vareps[:, 0, :], neghalf[:, :], ALU.pow).then_inc(rs_done, 1)
                        if st.out and h == 5 and t == 2:
                            pool.wait_ge(ve2_done, s)
                            g.tensor_tensor(rstd[:, 1, :], vareps[:, 1, :], neghalf[:, :], ALU.pow).then_inc(rs2_done, 1)
                        if st.out and h == 6 and t == 3:
                            pool.wait_ge(yln_done, s)
                            g.tensor_tensor(x2[1 - st.par][:, :, :], x2[1 - st.par][:, :, :],
                                            b2row[:, None, :].broadcast_to([P, NT, D]), ALU.add).then_inc(x2b_done, 1)
                        if st.sm and t >= 1:
                            pool.wait_ge(e_done, s * H * NT + h * NT + t + 1)
                            if t == 1 and h % G == 0:
                                wait(pool, l_full, s * NG + h // G)
                            if t > 1:
                                pool.wait_ge(es_done, s * 3 * H + 3 * h + t - 1)
                            first = E[:, h, 0, :] if t == 1 else esum[:, h % G, :]
                            g.tensor_tensor(esum[:, h % G, :], first, E[:, h, t, :], ALU.add).then_inc(es_done, 1)
                        task = TASKS_F.get((h, t), "")
                        if st.ffn and task.startswith("H"):
                            f = int(task[1])
                            pool.wait_ge(hh_done, (s - 2) * NF + f + 1)
                            g.tensor_tensor(hl[:, f, :], hf, hh[:, f, :], ALU.subtract).then_inc(hl_done, 1)
            steps(pool, step)

        @block.scalar
        def _(act):
            a = nc.scalar
            act.wait_ge(w_at, 16 * N_AT)
            for j in range(2):
                if j:
                    act.wait_ge(su_act, 1)
                a.activation(wabs, Ef[:, 2048 * j:2048 * (j + 1)], ACT.Abs, accum_out=gsum[:, j:j + 1]).then_inc(su_act, 1)

            def step(st):
                s = st.s
                for h in range(SLOTS):
                    for t in range(SEGS):
                        if st.sm:
                            n = s * H * NT + h * NT + t
                            if t == 0:
                                wait(act, pv_full, (s - 1) * NG * NT + (h // G + 1) * NT)
                                wait(act, es_done, (s - 1) * 3 * H + 3 * h + 3)
                            act.wait_ge(st_full, n + 1)
                            a.activation(E[:, h, t, :], ST[t % 2][:, :], ACT.Exp, scale=SCALE).then_inc(e_done, 1)
                        task = TASKS_A.get((h, t), "")
                        if task and st.has_a(task):
                            n = a_index(st, task)
                            act_a_task(st, task, n)
                        task = TASKS_F.get((h, t), "")
                        if task and st.has_f(task):
                            act_f_task(st, task, f_index(st, task))

            def act_a_task(st, task, n):
                kind = task[0]
                b = st.s + 1
                if kind in "XKCVR":
                    act.wait_ge(ga_full, n + 1)
                if kind == "X":
                    a.activation(xT[:, int(task[1]), :], GA[:, :], ACT.Copy).then_inc(ga_free, 1)
                elif kind == "K":
                    wait(act, k_done, 2 * b)
                    a.activation(kf[:, :], GA[:, :], ACT.Identity, bias=bk[:, 0:1]).then_inc(ga_free, 1)
                elif kind == "C":
                    wait(act, c_done, 2 * b)
                    a.activation(cf, GA[0:KQ, :], ACT.Identity, bias=bc[0:KQ, 0:1]).then_inc(ga_free, 1)
                elif kind == "V":
                    wait(act, pv_full, (st.s) * NG * NT)
                    a.activation(V[1 - st.par][:, :, :].rearrange("p t c -> p (t c)"), GA[:, 0:NT * DC],
                                 ACT.Copy).then_inc(ga_free, 1)
                elif kind == "R":
                    gr = int(task[1])
                    if gr == 1:
                        wait(act, st_full, st.s * H * NT)
                    else:
                        wait(act, st_full, st.s * H * NT + G * NT if st.sm else 0)
                    for j in range(G):
                        last = a.activation(QB[W:W + G, gr * G + j, :], GA[W:W + G, :], ACT.Copy,
                                            scale=headmask[W:W + G, j:j + 1])
                    last.then_inc(ga_free, 1)
                elif kind == "Q":
                    h = int(task[1])
                    act.wait_ge(ga_full, n + 1)
                    if st.sm:
                        wait(act, st_full, st.s * H * NT + (h + 1) * NT)
                        wait(act, mx_full, st.s * H * NT + (h + 1) * NT)
                    a.activation(QA[:, h, :], GA[:, :], ACT.Copy).then_inc(qh_done, 1)
                    a.activation(QB[0:W, h, :], GA[0:W, :], ACT.Copy).then_inc(qh_done, 1)

            def act_f_task(st, task, n):
                kind = task[0]
                if kind == "T":
                    act.wait_ge(gf_full, n + 1)
                    a.activation(yh[:, int(task[1]), :], GF[:, :], ACT.Copy).then_inc(yh_done, 1)
                elif kind == "H":
                    f = int(task[1])
                    act.wait_ge(gf_full, n + 1)
                    if f:
                        act.wait_ge(hl_done, (st.s - 2) * NF + f)
                    if f == 0:
                        for i in range(2):
                            act.wait_ge(o_sent[i], 8 * NT * (st.s - 2) + 16)
                    a.activation(hf, GF[:, :], ACT.Relu, bias=b1col[:, f:f + 1]).then_inc(gf_free, 1)

            steps(act, step)

        @block.vector
        def _(dve):
            v = nc.vector
            done = [0]

            def su(ins):
                done[0] += 1
                ins.then_inc(su_dve, 1)
            dve.wait_ge(memz, 2)
            v.memset(bc[3 * DC:3 * DC + 2, :], 1.0)
            for i in range(2):
                v.memset(KB[i][W:W + G, :].bitcast(F32), 1.0)
            dve.wait_ge(cst, 6)
            su(v.tensor_copy(identr[:, :], ident[:, :]))
            dve.wait_ge(w_at, 16 * N_AT)
            dve.wait_ge(su_pe, 1)
            tq = bank[0][:, 0:H * DC].rearrange("p (h c) -> p h c", h=H)
            tk = bank[0][:, H * DC:2 * H * DC].rearrange("p (h c) -> p h c", h=H)
            for j in range(3):
                v.tensor_copy(LQ[:, :, j * DC:(j + 1) * DC], tq)
            for j in range(2):
                v.tensor_copy(LQ[:, :, 3 * DC + j], colb[:, 0, :])
            v.tensor_copy(RK[:, :, 0:DC], tk)
            v.tensor_copy(RK[:, :, DC], colb[:, 1, :])
            v.tensor_copy(uvT, bank[1][:, 0:H * DC].rearrange("p (h c) -> p h c", h=H))
            su(v.tensor_copy(buvb, colb[:, 2, :, None].broadcast_to([P, H, P])))
            dve.wait_ge(su_pe, 2)
            ap = bank[2][0:KQ, 0:H * (DC + 1)].rearrange("p (h c) -> p h c", h=H)
            su(v.tensor_copy(AF[:, :, 0:DC], ap[:, :, 0:DC]))
            su(v.tensor_copy(AF[:, :, W], ap[:, :, DC]))
            dve.wait_ge(su_dve, 4)
            su(v.tensor_copy(AQ[:, :, 0, :], AF[:, :, 0:W]))
            su(v.tensor_copy(AC[:, :], AF[:, :, W]))
            dve.wait_ge(su_dve, 6)
            v.tensor_tensor(alr[:, :, 0:W], AF[:, :, 0:W], AQ[:, :, 0, :], ALU.subtract)
            su(v.tensor_tensor(alr[:, :, W], AF[:, :, W], AC[:, :], ALU.subtract))
            dve.wait_ge(su_dve, 7)
            lo = slice(2 * DC, 3 * DC)
            su(v.tensor_copy(AQ[lo, :, 0, :], alr[lo, :, 0:W]))
            su(v.tensor_copy(AC[lo, :], alr[lo, :, W]))
            dve.wait_ge(su_pe, 3)
            v.tensor_copy(M[:, 0, :], bank[3][:, 0:D])
            v.tensor_copy(M[:, 1, :], bank[3][:, D:2 * D])
            su(v.tensor_tensor(battn[:, :], bank[4][:, 0:D], bot, ALU.add))
            dve.wait_ge(row_sent, 32)
            v.tensor_copy(AQ[:, :, 1, :], AQ[:, :, 0, :])
            dve.wait_ge(su_pe, 4)
            su(v.tensor_scalar(gcol, bank[5][:, 0:2], 1.0 / (F * D), EPS, ALU.mult, ALU.add))
            dve.wait_ge(su_dve, 11)
            su(v.reciprocal(grec, gcol))
            dve.wait_ge(su_dve, 12)
            for j in range(2):
                wj = Ef[:, 2048 * j:2048 * (j + 1)]
                su(v.tensor_scalar(wj, wj, grec[:, j:j + 1], MAGIC, ALU.mult, ALU.add))
                dve.wait_ge(su_dve, done[0])
                su(v.tensor_scalar(wj, wj, -MAGIC, 1.0, ALU.add, ALU.min))
            assert done[0] == 16
            for i in range(8):
                dve.wait_ge(su_pe, 5 + i)
                if i < 4:
                    dst = w1T[:, i // 2, (i % 2) * 512:(i % 2 + 1) * 512]
                else:
                    dst = w2T[:, 2 * (i - 4):2 * (i - 4) + 2, :].rearrange("p n d -> p (n d)")
                su(v.tensor_scalar(dst, bank[i][:, :], -1.0, None, ALU.max))

            def ln_stats(src, which, ready, made, mvd, ved, b):
                ready()
                for t in range(NT):
                    last = v.bn_stats(stats[:, t, :], src[:, t, :])
                last.then_inc(made, 1)
                dve.wait_ge(made, b + 1)
                v.memset(carrier[0:1, which:which + 1], 0.0)
                for t in range(NT):
                    last = v.bn_aggr(mv[:, which, t, :], stats[:, t, :])
                last.then_inc(mvd, 1)
                dve.wait_ge(mvd, b + 1)
                v.tensor_scalar(vareps[:, which, :], mv[:, which, :, 1], EPS, None, ALU.add).then_inc(ved, 1)

            def step(st):
                s = st.s
                for h in range(SLOTS):
                    for t in range(SEGS):
                        task = TASKS_A.get((h, t), "")
                        if task and st.has_a(task):
                            dve_a_task(st, task, a_index(st, task))
                        if (h >= 2 and st.qk) or (h < 2 and st.sm):
                            b, head = (s + 1, h - 2) if h >= 2 else (s, h + 6)
                            if t == 0:
                                wait(dve, mf_done, (b - 1) * NG + head // G + 1)
                            dve.wait_ge(mx_full, b * H * NT + head * NT + t + 1)
                            v.reduce_max(rowmax[:, head, t:t + 1], MX[t % 2][:, :], AX.X).then_inc(mx_done, 1)
                        task = TASKS_F.get((h, t), "")
                        if task and st.has_f(task):
                            dve_f_task(st, task, f_index(st, task))
                        if (h == 2 and st.out) or (h == 6 and st.sm):
                            b, gr = (s - 1, 1) if h == 2 else (s, 0)
                            dve.wait_ge(l_full, b * NG + gr + 1)
                            c = slice(t * P, (t + 1) * P)
                            if t == 0 and gr == 0:
                                wait(dve, gf_full, f_index(st, "O1") + 1 if st.out else 0)
                            if t == 0 and gr == 1 and st.qk:
                                dve.wait_ge(c_done, 2 * (s + 1) + 2)
                            v.reciprocal(un[:, gr, c], L[:, c]).then_inc(rec_done, 1)
                        if (h == 3 and t == 2 and st.out) or (h == 7 and t == 2 and st.sm):
                            b, gr = (s - 1, 1) if h == 3 else (s, 0)
                            dve.wait_ge(pv_full, (b * NG + gr + 1) * NT)
                            dve.wait_ge(rec_done, (b * NG + gr + 1) * 4)
                            v.tensor_tensor(un[:, gr, :], U[:, :], un[:, gr, :], ALU.mult).then_inc(un_done, 1)
                        if st.ln and (h, t) == (4, 1):
                            ln_stats(xln, 0, lambda: dve.wait_ge(x_in, (s + 3) * 16), st_done, mv_done, ve_done, s + 2)
                        if st.ln and (h, t) == (5, 3):
                            dve.wait_ge(rs_done, s + 3)
                            for i in range(NT):
                                last = v.tensor_scalar(xln[:, i, :], xln[:, i, :], mv[:, 0, i, 0:1],
                                                       rstd[:, 0, i:i + 1], ALU.subtract, ALU.mult)
                            last.then_inc(xln_done, 1)
                        if st.out and (h, t) == (5, 1):
                            ln_stats(x2[1 - st.par], 1, lambda: dve.wait_ge(gf_free, f_index(st, "O1") + 1),
                                     st2_done, mv2_done, ve2_done, s - 1)
                        if st.out and (h, t) == (6, 0):
                            dve.wait_ge(rs2_done, s)
                            if st.qk:
                                dve.wait_ge(ga_full, a_index(st, "C") + 1)
                            for i in range(NT):
                                last = v.tensor_scalar(yln[:, i, :], x2[1 - st.par][:, i, :], mv[:, 1, i, 0:1],
                                                       rstd[:, 1, i:i + 1], ALU.subtract, ALU.mult)
                            last.then_inc(yln_done, 1)

            def dve_a_task(st, task, n):
                kind = task[0]
                b, p = st.s + 1, 1 - st.par
                if kind == "K":
                    dve.wait_ge(ga_free, n + 1)
                    wait(dve, st_full, (b - 1) * H * NT)
                    v.tensor_copy(KA[p][:, :], kf[:, :]).then_inc(k_done, 1)
                    dve.wait_ge(k_done, 2 * b + 1)
                    v.tensor_tensor(KB[p][0:W, :], kf[0:W, :], KA[p][0:W, :], ALU.subtract).then_inc(k_done, 1)
                elif kind == "C":
                    dve.wait_ge(ga_free, n + 1)
                    v.tensor_copy(cq[0:KQ, :], cf).then_inc(c_done, 1)
                    dve.wait_ge(c_done, 2 * b + 1)
                    mid = slice(DC, 2 * DC)
                    v.tensor_tensor(cq[mid, :], cf[mid, :], cq[mid, :], ALU.subtract).then_inc(c_done, 1)
                elif kind == "S":
                    dve.wait_ge(ga_full, n + 1)
                    v.tensor_copy(const[p][:, :, :].rearrange("p t h -> p (t h)"), GA[:, 0:NT * H]).then_inc(ga_free, 1)
                elif kind == "Q":
                    h = int(task[1])
                    dve.wait_ge(qh_done, b * 2 * H + 2 * h + 2)
                    v.tensor_tensor(QA[W:2 * W, h, :], GA[W:2 * W, :], QA[W:2 * W, h, :],
                                    ALU.subtract).then_inc(ga_free, 1)

            def dve_f_task(st, task, n):
                kind = task[0]
                if kind == "O":
                    i = int(task[1])
                    dve.wait_ge(gf_full, n + 1)
                    dve.wait_ge(xb_done, st.s)
                    two = x2[1 - st.par][:, 2 * i:2 * i + 2, :].rearrange("p t d -> p (t d)")
                    v.tensor_tensor(two, GF[:, :], two, ALU.add).then_inc(gf_free, 1)
                elif kind == "T":
                    k = int(task[1])
                    dve.wait_ge(yh_done, (st.s - 1) * KD + k + 1)
                    v.tensor_tensor(yl[:, k, :], GF[:, :], yh[:, k, :], ALU.subtract).then_inc(gf_free, 1)
                elif kind == "H":
                    f = int(task[1])
                    dve.wait_ge(gf_free, n + 1)
                    v.tensor_copy(hh[:, f, :], hf).then_inc(hh_done, 1)
                elif kind == "Y":
                    i = int(task[1])
                    dve.wait_ge(gf_full, n + 1)
                    if i == 0:
                        dve.wait_ge(x2b_done, st.s - 1)
                    if i == 0:
                        dve.wait_ge(hl_done, (st.s - 1) * NF)
                    if i >= 2:
                        dve.wait_ge(o_sent[i % 2], 8 * NT * (st.s - 2) + 32)
                    v.tensor_tensor(ob[:, i % 2, :], GF[:, 0:D], x2[st.par][:, i, :], ALU.add).then_inc(gf_free, 1)

            steps(dve, step)

        @block.tensor
        def _(pe):
            mm = nc.tensor.matmul
            tr = nc.tensor.transpose
            pe.wait_ge(cst, 6)
            pe.wait_ge(w_at, 16 * N_AT)
            for j, (w, bk_) in enumerate(((wuq, bank[0]), (wuk, bank[0]), (wuv, bank[1]))):
                for h in range(H):
                    c = (j % 2) * H * DC + h * DC
                    last = tr(bk_[:, c:c + DC], w[:, h * DK:(h + 1) * DK], ident[0:DC, 0:DC])
            last.then_inc(su_pe, 1)
            pe.wait_ge(su_dve, 2)
            for h in range(H):
                last = mm(bank[2][0:KQ, h * (DC + 1):(h + 1) * (DC + 1)], LQ[:, h, :], RK[:, h, :], start=True, stop=True)
            last.then_inc(su_pe, 1)
            for h in range(H):
                r = (h % G) * DC
                mm(bank[3][r:r + DC, (h // G) * D:(h // G + 1) * D], uvT[:, h, :], wo[:, h, :], start=True, stop=True)
            for h in range(H):
                last = mm(bank[4][:, 0:D], buvb[:, h, :], wo[:, h, :], start=(h == 0), stop=(h == H - 1))
            last.then_inc(su_pe, 1)
            pe.wait_ge(su_act, 2)
            mm(bank[5][:, 0:2], ones128, gsum, start=True, stop=True).then_inc(su_pe, 1)
            pe.wait_ge(su_dve, 16)
            for i in range(8):
                for j in range(4):
                    if i < 4:
                        src = w1n[:, (i % 2) * 4 + j, (i // 2) * P:(i // 2 + 1) * P]
                    else:
                        n = 2 * (i - 4) + j // 2
                        src = w2n[:, j % 2, n * P:(n + 1) * P]
                    last = tr(bank[i][:, j * P:(j + 1) * P], src, ident[:, :])
                last.then_inc(su_pe, 1)
            pe.wait_ge(su_dve, 24)
            pe.wait_ge(row_sent, 32)

            def step(st):
                s = st.s
                for h in range(SLOTS):
                    for t in range(SEGS):
                        tok = slice(t * P, (t + 1) * P)
                        if st.sm:
                            n = s * H * NT + h * NT + t
                            if (h, t) == (0, 0):
                                pe.wait_ge(ga_free, a_index(before(st), "R0") + 1)
                            if (h, t) == (G, 0):
                                pe.wait_ge(ga_free, a_index(st, "R1") + 1)
                            wait(pe, e_done, n - 1)
                            mm(ST[t % 2][:, :], KA[st.par][:, tok], QA[:, h, :], start=True, stop=False)
                            mm(ST[t % 2][:, :], KB[st.par][0:W + G, tok], QB[:, h, :], start=False,
                               stop=True).then_inc(st_full, 1)
                        task = TASKS_A.get((h, t), "")
                        if task and st.has_a(task):
                            pe_a_task(st, task, a_index(st, task))
                        if (h >= 2 and st.qk) or (h < 2 and st.sm):
                            b, head, p = (s + 1, h - 2, 1 - st.par) if h >= 2 else (s, h + 6, st.par)
                            if t == 0:
                                src = st if h >= 2 else before(st)
                                pe.wait_ge(ga_free, a_index(src, f"Q{head}") + 1)
                            wait(pe, mx_done, b * H * NT + head * NT + t - 1)
                            mm(MX[t % 2][:, :], QA[:, head, tok], KA[p][:, :], start=True, stop=True).then_inc(mx_full, 1)
                        task = TASKS_F.get((h, t), "")
                        if task and st.has_f(task):
                            pe_f_task(st, task, f_index(st, task))
                        if t == 1 and ((h < G and st.out) or (h >= G and st.sm)):
                            b, gr, p = (s - 1, 1, 1 - st.par) if h < G else (s, 0, st.par)
                            i = h % G
                            if i == 0:
                                pe.wait_ge(e_done, (b * H + (gr + 1) * G) * NT)
                                wait(pe, un_done, b * NG + gr)
                            for j in range(G):
                                r = slice(j * DC, (j + 1) * DC)
                                last = mm(U[r, :], V[p][:, i, :], E[:, gr * G + j, i, :], start=(i == 0),
                                          stop=(i == NT - 1))
                            last.then_inc(pv_full, 1)
                        if t == 2 and ((h == 0 and st.out) or (h == G and st.sm)):
                            b, gr = (s - 1, 1) if h == 0 else (s, 0)
                            pe.wait_ge(es_done, (b * H + (gr + 1) * G) * 3)
                            wait(pe, rec_done, (b * NG + gr) * 4)
                            for j in range(G):
                                r = slice(j * DC, (j + 1) * DC)
                                last = mm(L[r, :], ones32[:, :], esum[:, j, :], start=True, stop=True)
                            last.then_inc(l_full, 1)

            def pe_a_task(st, task, n):
                kind = task[0]
                b, p = st.s + 1, 1 - st.par
                wait(pe, ga_free, n)
                if kind == "X":
                    if task == "X0":
                        pe.wait_ge(xln_done, b + 1)
                    for t in range(NT):
                        last = tr(GA[:, t * P:(t + 1) * P], xln[:, t, int(task[1]) * P:(int(task[1]) + 1) * P], ident[:, :])
                elif kind in "KC":
                    w = wk if kind == "K" else wc
                    for k in range(KD):
                        last = mm(GA[0:(P if kind == "K" else KQ), :], w[:, k, :], xT[:, k, :], start=(k == 0), stop=(k == KD - 1))
                elif kind == "Q":
                    if task == "Q0":
                        pe.wait_ge(c_done, 2 * b + 2)
                    last = mm(GA[:, :], AQ[:, int(task[1]), :, :].rearrange("k a c -> k (a c)"), cq[0:KQ, :], start=True, stop=True)
                elif kind == "S":
                    for t in range(NT):
                        last = mm(GA[:, t * H:(t + 1) * H], cq[0:KQ, t * P:(t + 1) * P], AC[:, :], start=True, stop=True)
                elif kind == "V":
                    for t in range(NT):
                        last = mm(GA[:, t * DC:(t + 1) * DC], kf[0:DC, t * P:(t + 1) * P], ident[0:DC, 0:DC],
                                  start=True, stop=True)
                elif kind == "R":
                    gr = int(task[1])
                    pe.wait_ge(sh_done, (st.s if gr else b) * NG + gr + 1)
                    for t in range(NT):
                        last = mm(GA[0:W + G, t * P:(t + 1) * P], shift[:, t, :], identr[:, :], start=True, stop=True)
                last.then_inc(ga_full, 1)

            def pe_f_task(st, task, n):
                kind = task[0]
                wait(pe, gf_free, n)
                i = int(task[1])
                if kind == "O":
                    if i == 0:
                        pe.wait_ge(un_done, st.s * NG)
                    for t in range(2):
                        q = slice((2 * i + t) * P, (2 * i + t + 1) * P)
                        for gr in range(NG):
                            last = mm(GF[:, t * D:(t + 1) * D], un[:, gr, q], M[:, gr, :], start=(gr == 0), stop=(gr == NG - 1))
                elif kind == "T":
                    if i == 0:
                        pe.wait_ge(yln_done, st.s)
                    for t in range(NT):
                        last = tr(GF[:, t * P:(t + 1) * P], yln[:, t, i * P:(i + 1) * P], ident[:, :])
                elif kind == "H":
                    f = slice(i * P, (i + 1) * P)
                    for k in range(KD):
                        mm(GF[:, :], w1T[:, k, f], yh[:, k, :], start=(k == 0), stop=False)
                        last = mm(GF[:, :], w1T[:, k, f], yl[:, k, :], start=False, stop=(k == KD - 1))
                elif kind == "Y":
                    q = slice(i * P, (i + 1) * P)
                    if i == 0:
                        pe.wait_ge(hl_done, (st.s - 1) * NF)
                    for f in range(NF):
                        mm(GF[:, 0:D], hh[:, f, q], w2T[:, f, :], start=(f == 0), stop=False)
                        last = mm(GF[:, 0:D], hl[:, f, q], w2T[:, f, :], start=False, stop=(f == NF - 1))
                last.then_inc(gf_full, 1)

            steps(pe, step)


_INS = ["L0_attn_h_t", "L0_attn_W_DQ", "L0_attn_b_DQ", "L0_attn_W_UQ", "L0_attn_b_UQ", "L0_attn_W_DKV",
        "L0_attn_b_DKV", "L0_attn_W_UK", "L0_attn_b_UK", "L0_attn_W_UV", "L0_attn_b_UV", "L0_attn_W_QR",
        "L0_attn_b_QR", "L0_attn_W_KR", "L0_attn_b_KR", "L0_attn_W_O", "L0_attn_b_O", "L0_ffn_W1", "L0_ffn_b1",
        "L0_ffn_W2", "L0_ffn_b2"]


def kernel(**inputs):
    import numpy as _np
    import concourse.bacc as _bacc
    from concourse import mybir as _mybir
    from concourse.bass_utils import run_bass_kernel_spmd as _run

    nc = _bacc.Bacc("TRN2", target_bir_lowering=False, num_devices=1)
    arrays, args = {}, []
    for name in _INS:
        a = _np.ascontiguousarray(inputs[name])
        arrays[f"in_{name}"] = a
        args.append(nc.dram_tensor(f"in_{name}", a.shape, _mybir.dt.from_np(a.dtype), kind="ExternalInput").ap())
    shape = inputs["L0_attn_h_t"].shape
    args.append(nc.dram_tensor("out_0", shape, F32, kind="ExternalOutput").ap())
    layer_kernel(nc, *args)
    r = _run(nc, [arrays], core_ids=[0])
    return r.results[0]["out_0"]
```

```python
from contextlib import ExitStack

import concourse.bass as bass
from concourse import mybir

F32 = mybir.dt.float32
F32R = mybir.dt.float32r
ALU = mybir.AluOpType
ACT = mybir.ActivationFunctionType
AX = mybir.AxisListType

P = 128
SLOTS, SEGS = 8, 4

TASKS_A = {(0, 1): "X0", (0, 2): "X1", (0, 3): "K", (1, 2): "Q0", (2, 0): "S", (2, 1): "Q1", (2, 3): "R1",
           (3, 1): "Q2", (4, 1): "Q3", (5, 1): "Q4", (5, 3): "V", (6, 1): "Q5", (6, 3): "R0",
           (7, 1): "Q6", (7, 3): "Q7"}
TASKS_F = {(0, 0): "H0", (0, 2): "H1", (1, 0): "H2", (1, 2): "H3", (2, 0): "H4", (2, 2): "H5", (3, 0): "H6",
           (3, 2): "H7", (4, 1): "O0", (4, 2): "O1", (5, 0): "Y0", (5, 2): "Y1", (6, 0): "Y2", (6, 2): "T0",
           (7, 0): "T1", (7, 2): "Y3"}


class Step:

    def __init__(self, s, nb, parity=None):
        self.s, self.full = s, parity is not None
        self.par = parity if self.full else s % 2
        live = lambda b: self.full or 0 <= b < nb
        self.ln, self.qk, self.sm, self.out, self.ffn = (live(s + d) for d in ((2, 1, 0, -1, -2)))

    def has_a(self, task):
        return self.sm if task == "R1" else self.qk

    def has_f(self, task):
        return self.ffn if task[0] in "HY" else self.out


def layer_kernel(nc, x, W_DQ, b_DQ, W_UQ, b_UQ, W_DKV, b_DKV, W_UK, b_UK, W_UV, b_UV, W_QR, b_QR, W_KR, b_KR,
                 W_O, b_O, W1, b1, W2, b2, out):
    NB, S, D = x.shape
    DC = W_DQ.shape[1]
    DR = W_KR.shape[1]
    H = W_QR.shape[1] // DR
    DK = W_UQ.shape[1] // H
    F = W1.shape[0]
    KD = D // P
    NF = F // P
    NT = S // P
    W = DC + DR
    G = 4
    NG = H // G
    KQ = 3 * DC + 2
    SCALE = float(DK + DR) ** -0.5
    MAGIC = 1.5 * 2.0 ** 23
    EPS = 1e-5
    assert (S, D, DC, DR, DK, H) == (512, 256, 32, 32, 128, SLOTS) and NT == SEGS and F == 1024 and NB % 2 == 0

    ctx = ExitStack()
    with ctx:
        def sb(name, shape, dt=F32):
            return ctx.enter_context(nc.sbuf_tensor(name, shape, dt))

        def sem(name):
            return ctx.enter_context(nc.semaphore(name))

        bank = [ctx.enter_context(nc.psum_tensor(n, [P, 512], F32))
                for n in ("bST0", "bST1", "bMX0", "bMX1", "bU", "bL", "bGA", "bGF")]
        ST, MX, U, L, GA, GF = bank[0:2], bank[2:4], bank[4], bank[5], bank[6], bank[7]

        ident = sb("ident", [P, P])
        identr = sb("identr", [P, P], F32R)
        ones32 = sb("ones32", [P, 32])
        neghalf = sb("neghalf", [P, NT])
        headmask = sb("headmask", [P, G])
        wk = sb("wk", [P, KD, W + DC])
        bk = sb("bk", [P, 1])
        bc = sb("bc", [3 * DC, 1])
        AQ = sb("AQ", [KQ, H, 2, W], F32R)
        AC = sb("AC", [KQ, H], F32R)
        M = sb("M", [P, NG, D])
        battn = sb("battn", [P, D])
        b2row = sb("b2row", [P, D])
        b1col = sb("b1col", [P, NF])
        w1T = sb("w1T", [P, KD, F], F32R)
        w2T = sb("w2T", [P, NF, D], F32R)
        xln = sb("xln", [P, NT, D])
        xT = sb("xT", [P, KD, S])
        yln = xT[:, :, :].rearrange("p k s -> p (k s)").rearrange("p (t d) -> p t d", t=NT)
        kf = sb("kf", [P, S])
        cq = sb("cq", [P, S], F32R)
        KA = [sb(f"KA{i}", [P, S], F32R) for i in range(2)]
        KB = [sb(f"KB{i}", [P, S], F32R) for i in range(2)]
        V = [sb(f"V{i}", [P, NT, DC]) for i in range(2)]
        QA = sb("QA", [P, H, S], F32R)
        QB = sb("QB", [W + G, H, S], F32R)
        rowmax = sb("rowmax", [P, H, NT])
        const = [sb(f"const{i}", [P, NT, H]) for i in range(2)]
        mfull = sb("mfull", [P, G, NT])
        shift = sb("shift", [P, NT, W + G], F32R)
        E = sb("E", [P, H, NT, S])
        esum = sb("esum", [P, G, S])
        un = sb("un", [P, NG, S])
        x2 = [sb(f"x2_{i}", [P, NT, D]) for i in range(2)]
        stats = sb("stats", [P, NT, 6])
        mv = sb("mv", [P, 2, NT, 2])
        carrier = sb("carrier", [1, 2])
        vareps = sb("vareps", [P, 2, NT])
        rstd = sb("rstd", [P, 2, NT])
        yh = sb("yh", [P, KD, S], F32R)
        yl = sb("yl", [P, KD, S], F32R)
        hh = sb("hh", [P, NF, S], F32R)
        hl = sb("hl", [P, NF, S], F32R)
        ob = sb("ob", [P, 2, D])
        hf = ob[:, :, :].rearrange("p a d -> p (a d)")
        cf = un[0:3 * DC, 1, :]

        Ef = E[:, :, :, :].rearrange("p h t s -> p (h t s)")
        w1n = Ef[:, 0:2048].rearrange("p (n d) -> p n d", n=NF)
        w2n = Ef[:, 2048:4096].rearrange("p (n f) -> p n f", n=KD)
        wo = Ef[:, 4096:6144].rearrange("p (h n) -> p h n", h=H)
        wuq = Ef[0:DC, 6144:7168]
        wuk = Ef[0:DC, 7168:8192]
        wuv = Ef[0:DC, 8192:9216]
        LQ = Ef[:, 9216:9216 + H * KQ].rearrange("p (h c) -> p h c", h=H)
        RK = Ef[:, 10240:10240 + H * (DC + 1)].rearrange("p (h c) -> p h c", h=H)
        uvT = Ef[:, 10624:10880].rearrange("p (h c) -> p h c", h=H)
        buvb = Ef[:, 11008:12032].rearrange("p (h c) -> p h c", h=H)
        AF = Ef[0:KQ, 12032:12032 + H * (W + 1)].rearrange("p (h c) -> p h c", h=H)
        alr = Ef[0:KQ, 12608:12608 + H * (W + 1)].rearrange("p (h c) -> p h c", h=H)
        brow = Ef[0:H, 15910:15910 + 3 * P].rearrange("h (k p) -> h k p", k=3)
        b1row = Ef[0:H, 13696:13696 + P]
        ones128 = Ef[:, 13312:13440]
        bot = Ef[:, 13440:13696]
        wabs = Ef[:, 13824:15872]
        gsum = Ef[:, 15900:15902]
        gcol = Ef[:, 15902:15904]
        grec = Ef[:, 15904:15906]
        w_at = sem("w_at")
        w_ff = sem("w_ff")
        cst = sem("cst")
        su_pe = sem("su_pe")
        su_dve = sem("su_dve")
        su_act = sem("su_act")
        row_sent = sem("row_sent")
        x_in = sem("x_in")
        xln_done = sem("xln_done")
        ga_full = sem("ga_full")
        ga_free = sem("ga_free")
        gf_full = sem("gf_full")
        gf_free = sem("gf_free")
        cf_done = sem("cf_done")
        k_done = sem("k_done")
        c_done = sem("c_done")
        qh_done = sem("qh_done")
        mx_full = sem("mx_full")
        mx_done = sem("mx_done")
        mf_done = sem("mf_done")
        sh_done = sem("sh_done")
        st_full = sem("st_full")
        e_done = sem("e_done")
        es_done = sem("es_done")
        pv_full = sem("pv_full")
        l_full = sem("l_full")
        rec_done = sem("rec_done")
        un_done = sem("un_done")
        xr_in = sem("xr_in")
        xb_done = sem("xb_done")
        st_done = sem("st_done")
        st2_done = sem("st2_done")
        mv_done = sem("mv_done")
        mv2_done = sem("mv2_done")
        ve_done = sem("ve_done")
        ve2_done = sem("ve2_done")
        rs_done = sem("rs_done")
        rs2_done = sem("rs2_done")
        yln_done = sem("yln_done")
        x2b_done = sem("x2b_done")
        yh_done = sem("yh_done")
        hh_done = sem("hh_done")
        hl_done = sem("hl_done")
        o_sent = [sem(f"o_sent{i}") for i in range(2)]

        def wait(eng, s, value):
            if isinstance(value, int) and value <= 0:
                return
            eng.wait_ge(s, value)

        N_AT, N_FF = 23, 4

        def a_index(st, task):
            mine = [t for t in TASKS_A.values() if st.has_a(t)].index(task)
            return mine if not st.full and st.s == -1 else st.s * len(TASKS_A) + (len(TASKS_A) - 1) + mine

        def f_index(st, task):
            mine = [t for t in TASKS_F.values() if st.has_f(t)].index(task)
            return mine if not st.full and st.s == 1 else (st.s - 2) * len(TASKS_F) + 4 + mine

        def before(st):
            return Step(st.s - 1, NB, 1 - st.par) if st.full else Step(st.s - 1, NB)

        def f_after_prev(st, task):
            if st.full:
                mine = list(TASKS_F.values()).index(task)
                return (st.s - 3) * len(TASKS_F) + 4 + mine + 1
            p = Step(st.s - 1, NB)
            return f_index(p, task) + 1 if p.has_f(task) else 0

        def steps(eng, body, attention_weights=None, ffn_weights=None):
            body(Step(-2, NB))
            if attention_weights:
                attention_weights()
            body(Step(-1, NB))
            if ffn_weights:
                ffn_weights()
            body(Step(0, NB))
            body(Step(1, NB))
            with eng.Fori(1, NB // 2 - 1) as pair:
                body(Step(pair * 2, NB, 0))
                body(Step(pair * 2 + 1, NB, 1))
            for s in range(NB - 2, NB + 2):
                body(Step(s, NB))

        block = ctx.enter_context(nc.Block())

        @block.sync
        def _(sp):
            def loads(arrived):
                def at(dst, src):
                    with nc.allow_non_contiguous_dma(reason="short bias columns, once"):
                        sp.dma_start(dst, src).then_inc(arrived, 16)
                return at
            at = loads(w_at)
            sp.dma_start(xln[:, :, :], x[0].rearrange("(t p) d -> p t d", p=P)).then_inc(x_in, 16)
            for j, w in enumerate((W_DKV, W_KR, W_DQ)):
                at(wk[:, :, j * DC:(j + 1) * DC], w.rearrange("(k p) c -> p k c", p=P))
            at(wuq, W_UQ)
            at(wuk, W_UK)
            at(wuv, W_UV)
            for j in range(2):
                at(bk[j * W:j * W + DC, :], b_DKV.rearrange("(c a) -> c a", a=1))
                at(bk[j * W + DC:(j + 1) * W, :], b_KR.rearrange("(c a) -> c a", a=1))
            for j in range(3):
                at(bc[j * DC:(j + 1) * DC, :], b_DQ.rearrange("(c a) -> c a", a=1))
                at(AF[j * DC:(j + 1) * DC, :, DC:W], W_QR.rearrange("c (h r) -> c h r", h=H))
            for j in range(2):
                at(AF[3 * DC + j:3 * DC + j + 1, :, DC:W], b_QR.rearrange("(a h r) -> a h r", a=1, h=H))
            for j, b in enumerate((b_UQ, b_UK, b_UV)):
                at(brow[:, j, :], b.rearrange("(h p) -> h p", p=P))
            at(wo, W_O.rearrange("(h p) n -> p h n", p=P))
            at(bot, b_O.rearrange("(a n) -> a n", a=1).broadcast_to([P, D]))
            at = loads(w_ff)
            at(w1n, W1.rearrange("(n p) d -> p n d", p=P))
            at(w2n, W2.rearrange("(n p) f -> p n f", p=P))
            at(b1row, b1.rearrange("(n p) -> n p", p=P))
            at(b2row[:, :], b2.rearrange("(a n) -> a n", a=1).broadcast_to([P, D]))
            sp.wait_ge(su_dve, 9)
            sp.dma_start(AQ[KQ - 1:KQ, :, 0, :].bitcast(F32), alr[KQ - 1:KQ, :, 0:W]).then_inc(row_sent, 16)
            with nc.allow_non_contiguous_dma(reason="eight numbers"):
                sp.dma_start(AC[KQ - 1:KQ, :].bitcast(F32), alr[KQ - 1:KQ, :, W]).then_inc(row_sent, 16)

            def step(st):
                s = st.s
                if st.out:
                    wait(sp, gf_free, f_after_prev(st, "Y3"))
                    b = s - 1
                    sp.dma_start(x2[1 - st.par][:, :, :],
                                 x[bass.ds(b, 1)].rearrange("a (t p) d -> p (a t) d", p=P)).then_inc(xr_in, 16)
                if st.ln and not (not st.full and s == -2):
                    wait(sp, ga_full, a_index(st, "X1") + 1)
                    sp.dma_start(xln[:, :, :],
                                 x[bass.ds(s + 2, 1)].rearrange("a (t p) d -> p (a t) d", p=P)).then_inc(x_in, 16)
                if st.ffn:
                    for t in range(NT):
                        sp.wait_ge(gf_free, f_index(st, f"Y{t}") + 1)
                        sp.dma_start(out[bass.ds(s - 2, 1), t * P:(t + 1) * P, :].rearrange("a p d -> p (a d)"),
                                     ob[:, t % 2, :]).then_inc(o_sent[t % 2], 16)
            steps(sp, step)
            for i in range(2):
                sp.wait_ge(o_sent[i], 8 * NB * NT + 16)

        @block.gpsimd
        def _(pool):
            g = nc.gpsimd
            g.memset(ident[:, :], 0.0).then_inc(cst, 1)
            g.memset(headmask[:, :], 0.0).then_inc(cst, 1)
            pool.wait_ge(cst, 2)
            g.affine_select(out=ident[:, :], in_=ident[:, :], compare_op=ALU.not_equal, fill=1.0, base=0,
                            pattern=[[-1, P]], channel_multiplier=1).then_inc(cst, 1)
            g.affine_select(out=headmask[:, :], in_=headmask[:, :], compare_op=ALU.not_equal, fill=1.0, base=-W,
                            pattern=[[-1, G]], channel_multiplier=1).then_inc(cst, 1)
            g.memset(ones32[:, :], 1.0).then_inc(o_sent[0], 16)
            g.memset(neghalf[:, :], -0.5).then_inc(o_sent[1], 16)
            g.memset(ones128, 1.0).then_inc(cst, 1)
            g.memset(shift[:, :, :].bitcast(F32), 0.0).then_inc(cst, 1)
            pool.wait_ge(cst, 6)

            def step(st):
                s = st.s
                for h in range(SLOTS):
                    if st.out and h == 0:
                        pool.wait_ge(xr_in, s * 16)
                        g.tensor_tensor(x2[1 - st.par][:, :, :], x2[1 - st.par][:, :, :],
                                        battn[:, None, :].broadcast_to([P, NT, D]), ALU.add).then_inc(xb_done, 1)
                    for t in range(SEGS):
                        if st.ln and h == 4 and t == 2:
                            pool.wait_ge(ve_done, s + 3)
                            g.tensor_tensor(rstd[:, 0, :], vareps[:, 0, :], neghalf[:, :], ALU.pow).then_inc(rs_done, 1)
                        if st.out and h == 5 and t == 2:
                            pool.wait_ge(ve2_done, s)
                            g.tensor_tensor(rstd[:, 1, :], vareps[:, 1, :], neghalf[:, :], ALU.pow).then_inc(rs2_done, 1)
                        if st.out and h == 6 and t == 3:
                            pool.wait_ge(yln_done, s)
                            g.tensor_tensor(x2[1 - st.par][:, :, :], x2[1 - st.par][:, :, :],
                                            b2row[:, None, :].broadcast_to([P, NT, D]), ALU.add).then_inc(x2b_done, 1)
                        if st.sm and t >= 1:
                            pool.wait_ge(e_done, s * H * NT + h * NT + t + 1)
                            if t == 1 and h % G == 0:
                                wait(pool, l_full, s * NG + h // G)
                            if t > 1:
                                pool.wait_ge(es_done, s * 3 * H + 3 * h + t - 1)
                            first = E[:, h, 0, :] if t == 1 else esum[:, h % G, :]
                            g.tensor_tensor(esum[:, h % G, :], first, E[:, h, t, :], ALU.add).then_inc(es_done, 1)
                        task = TASKS_F.get((h, t), "")
                        if st.ffn and st.sm and task.startswith("H"):
                            f = int(task[1])
                            pool.wait_ge(hh_done, (s - 2) * NF + f + 1)
                            g.tensor_tensor(hl[:, f, :], hf, hh[:, f, :], ALU.subtract).then_inc(hl_done, 1)
            steps(pool, step)

        @block.scalar
        def _(act):
            a = nc.scalar
            def ffn_weights():
                act.wait_ge(w_ff, 16 * N_FF)
                for j in range(2):
                    if j:
                        act.wait_ge(su_act, 1)
                    a.activation(wabs, Ef[:, 2048 * j:2048 * (j + 1)], ACT.Abs,
                                 accum_out=gsum[:, j:j + 1]).then_inc(su_act, 1)

            def step(st):
                s = st.s
                for h in range(SLOTS):
                    for t in range(SEGS):
                        if st.sm:
                            n = s * H * NT + h * NT + t
                            if t == 0:
                                wait(act, pv_full, (s - 1) * NG * NT + (h // G + 1) * NT)
                                wait(act, es_done, (s - 1) * 3 * H + 3 * h + 3)
                            act.wait_ge(st_full, n + 1)
                            a.activation(E[:, h, t, :], ST[t % 2][:, :], ACT.Exp, scale=SCALE).then_inc(e_done, 1)
                        task = TASKS_A.get((h, t), "")
                        if task and st.has_a(task):
                            n = a_index(st, task)
                            act_a_task(st, task, n)
                        task = TASKS_F.get((h, t), "")
                        if task and st.has_f(task):
                            act_f_task(st, task, f_index(st, task))

            def act_a_task(st, task, n):
                kind = task[0]
                b = st.s + 1
                if kind in "XKVR":
                    act.wait_ge(ga_full, n + 1)
                if kind == "X":
                    a.activation(xT[:, int(task[1]), :], GA[:, :], ACT.Copy).then_inc(ga_free, 1)
                elif kind == "K":
                    wait(act, c_done, 2 * b)
                    for j in range(3):
                        q = slice(j * DC, (j + 1) * DC)
                        last = a.activation(cf[q, :], GA[W:W + DC, :], ACT.Identity, bias=bc[q, 0:1])
                    last.then_inc(cf_done, 1)
                    wait(act, k_done, 2 * b)
                    for j in range(2):
                        q = slice(j * W, (j + 1) * W)
                        last = a.activation(kf[q, :], GA[0:W, :], ACT.Identity, bias=bk[q, 0:1])
                    last.then_inc(ga_free, 1)
                elif kind == "V":
                    wait(act, pv_full, (st.s) * NG * NT)
                    a.activation(V[1 - st.par][:, :, :].rearrange("p t c -> p (t c)"), GA[:, 0:NT * DC],
                                 ACT.Copy).then_inc(ga_free, 1)
                elif kind == "R":
                    gr = int(task[1])
                    if gr == 1:
                        wait(act, st_full, st.s * H * NT)
                    else:
                        wait(act, st_full, st.s * H * NT + G * NT if st.sm else 0)
                    for j in range(G):
                        last = a.activation(QB[W:W + G, gr * G + j, :], GA[W:W + G, :], ACT.Copy,
                                            scale=headmask[W:W + G, j:j + 1])
                    last.then_inc(ga_free, 1)
                elif kind == "Q":
                    h = int(task[1])
                    act.wait_ge(ga_full, n + 1)
                    if st.sm:
                        wait(act, st_full, st.s * H * NT + (h + 1) * NT)
                        wait(act, mx_full, st.s * H * NT + (h + 1) * NT)
                    a.activation(QA[:, h, :], GA[:, :], ACT.Copy).then_inc(qh_done, 1)
                    a.activation(QB[0:W, h, :], GA[0:W, :], ACT.Copy).then_inc(qh_done, 1)

            def act_f_task(st, task, n):
                kind = task[0]
                if kind == "T":
                    act.wait_ge(gf_full, n + 1)
                    a.activation(yh[:, int(task[1]), :], GF[:, :], ACT.Copy).then_inc(yh_done, 1)
                elif kind == "H":
                    f = int(task[1])
                    act.wait_ge(gf_full, n + 1)
                    if f:
                        act.wait_ge(hl_done, (st.s - 2) * NF + f)
                    if f == 0:
                        for i in range(2):
                            act.wait_ge(o_sent[i], 8 * NT * (st.s - 2) + 16)
                    a.activation(hf, GF[:, :], ACT.Relu, bias=b1col[:, f:f + 1]).then_inc(gf_free, 1)

            steps(act, step, None, ffn_weights)

        @block.vector
        def _(dve):
            v = nc.vector
            done = [0]

            def su(ins):
                done[0] += 1
                ins.then_inc(su_dve, 1)
            v.memset(cq[3 * DC:KQ, :].bitcast(F32), 1.0)
            for i in range(2):
                v.memset(KB[i][W:W + G, :].bitcast(F32), 1.0)
            def attention_weights():
                dve.wait_ge(cst, 6)
                dve.wait_ge(w_at, 16 * N_AT)
                su(v.tensor_copy(identr[:, :], ident[:, :]))
                dve.wait_ge(su_pe, 1)
                tq = bank[0][:, 0:H * DC].rearrange("p (h c) -> p h c", h=H)
                tk = bank[0][:, H * DC:2 * H * DC].rearrange("p (h c) -> p h c", h=H)
                tv = bank[1][:, 0:H * DC].rearrange("p (h c) -> p h c", h=H)
                tb = bank[1][:, H * DC:H * DC + 3 * H].rearrange("p (k h) -> p k h", k=3)
                for j in range(3):
                    v.tensor_copy(LQ[:, :, j * DC:(j + 1) * DC], tq)
                for j in range(2):
                    v.tensor_copy(LQ[:, :, 3 * DC + j], tb[:, 0, :])
                v.tensor_copy(RK[:, :, 0:DC], tk)
                v.tensor_copy(RK[:, :, DC], tb[:, 1, :])
                v.tensor_copy(uvT, tv)
                su(v.tensor_copy(buvb, tb[:, 2, :, None].broadcast_to([P, H, P])))
                dve.wait_ge(su_pe, 2)
                prod = bank[2][0:KQ, 0:H * (DC + 1)].rearrange("p (h c) -> p h c", h=H)
                su(v.tensor_copy(AF[:, :, 0:DC], prod[:, :, 0:DC]))
                su(v.tensor_copy(AF[:, :, W], prod[:, :, DC]))
                dve.wait_ge(su_dve, 4)
                su(v.tensor_copy(AQ[:, :, 0, :], AF[:, :, 0:W]))
                su(v.tensor_copy(AC[:, :], AF[:, :, W]))
                dve.wait_ge(su_dve, 6)
                v.tensor_tensor(alr[:, :, 0:W], AF[:, :, 0:W], AQ[:, :, 0, :], ALU.subtract)
                su(v.tensor_tensor(alr[:, :, W], AF[:, :, W], AC[:, :], ALU.subtract))
                dve.wait_ge(su_dve, 7)
                lo = slice(2 * DC, 3 * DC)
                su(v.tensor_copy(AQ[lo, :, 0, :], alr[lo, :, 0:W]))
                su(v.tensor_copy(AC[lo, :], alr[lo, :, W]))
                dve.wait_ge(su_pe, 3)
                v.tensor_copy(M[:, 0, :], bank[3][:, 0:D])
                v.tensor_copy(M[:, 1, :], bank[3][:, D:2 * D])
                su(v.tensor_tensor(battn[:, :], bank[4][:, 0:D], bot, ALU.add))
                dve.wait_ge(row_sent, 32)
                su(v.tensor_copy(AQ[:, :, 1, :], AQ[:, :, 0, :]))

            def ffn_weights():
                dve.wait_ge(w_ff, 16 * N_FF)
                dve.wait_ge(su_pe, 4)
                v.tensor_copy(b1col[:, :], bank[5][:, NF:2 * NF])
                su(v.tensor_scalar(gcol, bank[5][:, 0:2], 1.0 / (F * D), EPS, ALU.mult, ALU.add))
                dve.wait_ge(su_dve, 12)
                su(v.reciprocal(grec, gcol))
                dve.wait_ge(su_dve, 13)
                for j in range(2):
                    wj = Ef[:, 2048 * j:2048 * (j + 1)]
                    su(v.tensor_scalar(wj, wj, grec[:, j:j + 1], MAGIC, ALU.mult, ALU.add))
                    dve.wait_ge(su_dve, done[0])
                    su(v.tensor_scalar(wj, wj, -MAGIC, 1.0, ALU.add, ALU.min))
                for i in range(8):
                    dve.wait_ge(su_pe, 5 + i)
                    if i < 4:
                        dst = w1T[:, i // 2, (i % 2) * 512:(i % 2 + 1) * 512]
                    else:
                        dst = w2T[:, 2 * (i - 4):2 * (i - 4) + 2, :].rearrange("p n d -> p (n d)")
                    su(v.tensor_scalar(dst, bank[i][:, :], -1.0, None, ALU.max))

            def shift_group(b, par, gr, before_full):
                dve.wait_ge(mx_done, b * H * NT + (gr + 1) * G * NT)
                wait(dve, mf_done, b * NG + gr)
                c = const[par][:, :, gr * G:(gr + 1) * G].rearrange("p t h -> p h t")
                v.tensor_tensor(mfull[:, :, :], rowmax[:, gr * G:(gr + 1) * G, :], c, ALU.add).then_inc(mf_done, 1)
                dve.wait_ge(mf_done, b * NG + gr + 1)
                wait(dve, ga_full, before_full)
                v.tensor_tensor(shift[:, :, W:W + G].rearrange("p t h -> p h t"), c, mfull[:, :, :],
                                ALU.subtract).then_inc(sh_done, 1)

            def ln_stats(src, which, ready, made, mvd, ved, b):
                ready()
                for t in range(NT):
                    last = v.bn_stats(stats[:, t, :], src[:, t, :])
                last.then_inc(made, 1)
                dve.wait_ge(made, b + 1)
                v.memset(carrier[0:1, which:which + 1], 0.0)
                for t in range(NT):
                    last = v.bn_aggr(mv[:, which, t, :], stats[:, t, :])
                last.then_inc(mvd, 1)
                dve.wait_ge(mvd, b + 1)
                v.tensor_scalar(vareps[:, which, :], mv[:, which, :, 1], EPS, None, ALU.add).then_inc(ved, 1)

            def step(st):
                s = st.s
                for h in range(SLOTS):
                    for t in range(SEGS):
                        task = TASKS_A.get((h, t), "")
                        if task and st.has_a(task) and task != "K":
                            dve_a_task(st, task, a_index(st, task))
                        if (h >= 2 and st.qk) or (h < 2 and st.sm):
                            b, head = (s + 1, h - 2) if h >= 2 else (s, h + 6)
                            if t == 0:
                                wait(dve, mf_done, (b - 1) * NG + head // G + 1)
                            dve.wait_ge(mx_full, b * H * NT + head * NT + t + 1)
                            v.reduce_max(rowmax[:, head, t:t + 1], MX[t % 2][:, :], AX.X).then_inc(mx_done, 1)
                        if st.qk and (h, t) == (1, 0):
                            dve_a_task(st, "K", a_index(st, "K"))
                        if st.sm and (h, t) == (2, 1):
                            shift_group(s, st.par, 1, a_index(before(st), "R0") + 1)
                        if st.qk and (h, t) == (6, 1):
                            shift_group(s + 1, 1 - st.par, 0, a_index(st, "R1") + 1 if st.sm else 0)
                        task = TASKS_F.get((h, t), "")
                        if task and st.has_f(task):
                            dve_f_task(st, task, f_index(st, task))
                        if (h == 2 and st.out) or (h == 6 and st.sm):
                            b, gr = (s - 1, 1) if h == 2 else (s, 0)
                            dve.wait_ge(l_full, b * NG + gr + 1)
                            c = slice(t * P, (t + 1) * P)
                            if t == 0 and gr == 0:
                                wait(dve, gf_full, f_index(st, "O1") + 1 if st.out else 0)
                            if t == 0 and gr == 1 and st.qk:
                                dve.wait_ge(c_done, 2 * (s + 1) + 2)
                            v.reciprocal(un[:, gr, c], L[:, c]).then_inc(rec_done, 1)
                        if (h == 3 and t == 2 and st.out) or (h == 7 and t == 2 and st.sm):
                            b, gr = (s - 1, 1) if h == 3 else (s, 0)
                            dve.wait_ge(pv_full, (b * NG + gr + 1) * NT)
                            dve.wait_ge(rec_done, (b * NG + gr + 1) * 4)
                            v.tensor_tensor(un[:, gr, :], U[:, :], un[:, gr, :], ALU.mult).then_inc(un_done, 1)
                        if st.ln and (h, t) == (4, 1):
                            ln_stats(xln, 0, lambda: dve.wait_ge(x_in, (s + 3) * 16), st_done, mv_done, ve_done, s + 2)
                        if st.ln and (h, t) == (5, 3):
                            dve.wait_ge(rs_done, s + 3)
                            for i in range(NT):
                                last = v.tensor_scalar(xln[:, i, :], xln[:, i, :], mv[:, 0, i, 0:1],
                                                       rstd[:, 0, i:i + 1], ALU.subtract, ALU.mult)
                            last.then_inc(xln_done, 1)
                        if st.out and (h, t) == (5, 1):
                            ln_stats(x2[1 - st.par], 1, lambda: dve.wait_ge(gf_free, f_index(st, "O1") + 1),
                                     st2_done, mv2_done, ve2_done, s - 1)
                        if st.out and (h, t) == (6, 0):
                            dve.wait_ge(rs2_done, s)
                            if st.qk:
                                dve.wait_ge(ga_full, a_index(st, "K") + 1)
                            for i in range(NT):
                                last = v.tensor_scalar(yln[:, i, :], x2[1 - st.par][:, i, :], mv[:, 1, i, 0:1],
                                                       rstd[:, 1, i:i + 1], ALU.subtract, ALU.mult)
                            last.then_inc(yln_done, 1)

            def dve_a_task(st, task, n):
                kind = task[0]
                b, p = st.s + 1, 1 - st.par
                if kind == "K":
                    dve.wait_ge(cf_done, b + 1)
                    v.tensor_copy(cq[0:3 * DC, :], cf).then_inc(c_done, 1)
                    dve.wait_ge(c_done, 2 * b + 1)
                    mid = slice(DC, 2 * DC)
                    v.tensor_tensor(cq[mid, :], cf[mid, :], cq[mid, :], ALU.subtract).then_inc(c_done, 1)
                    dve.wait_ge(ga_free, n + 1)
                    wait(dve, st_full, (b - 1) * H * NT)
                    v.tensor_copy(KA[p][:, :], kf[:, :]).then_inc(k_done, 1)
                    dve.wait_ge(k_done, 2 * b + 1)
                    v.tensor_tensor(KB[p][0:W, :], kf[0:W, :], KA[p][0:W, :], ALU.subtract).then_inc(k_done, 1)
                elif kind == "S":
                    dve.wait_ge(ga_full, n + 1)
                    v.tensor_copy(const[p][:, :, :].rearrange("p t h -> p (t h)"), GA[:, 0:NT * H]).then_inc(ga_free, 1)
                elif kind == "Q":
                    h = int(task[1])
                    dve.wait_ge(qh_done, b * 2 * H + 2 * h + 1)
                    v.tensor_tensor(QA[W:2 * W, h, :], GA[W:2 * W, :], QA[W:2 * W, h, :],
                                    ALU.subtract).then_inc(ga_free, 1)

            def dve_f_task(st, task, n):
                kind = task[0]
                if kind == "O":
                    i = int(task[1])
                    dve.wait_ge(gf_full, n + 1)
                    dve.wait_ge(xb_done, st.s)
                    two = x2[1 - st.par][:, 2 * i:2 * i + 2, :].rearrange("p t d -> p (t d)")
                    v.tensor_tensor(two, GF[:, :], two, ALU.add).then_inc(gf_free, 1)
                elif kind == "T":
                    k = int(task[1])
                    dve.wait_ge(yh_done, (st.s - 1) * KD + k + 1)
                    v.tensor_tensor(yl[:, k, :], GF[:, :], yh[:, k, :], ALU.subtract).then_inc(gf_free, 1)
                elif kind == "H":
                    f = int(task[1])
                    dve.wait_ge(gf_free, n + 1)
                    v.tensor_copy(hh[:, f, :], hf).then_inc(hh_done, 1)
                    if not st.sm:
                        dve.wait_ge(hh_done, (st.s - 2) * NF + f + 1)
                        v.tensor_tensor(hl[:, f, :], hf, hh[:, f, :], ALU.subtract).then_inc(hl_done, 1)
                elif kind == "Y":
                    i = int(task[1])
                    dve.wait_ge(gf_full, n + 1)
                    if i == 0:
                        dve.wait_ge(x2b_done, st.s - 1)
                    if i == 0:
                        dve.wait_ge(hl_done, (st.s - 1) * NF)
                    if i >= 2:
                        dve.wait_ge(o_sent[i % 2], 8 * NT * (st.s - 2) + 32)
                    v.tensor_tensor(ob[:, i % 2, :], GF[:, 0:D], x2[st.par][:, i, :], ALU.add).then_inc(gf_free, 1)

            steps(dve, step, attention_weights, ffn_weights)

        @block.tensor
        def _(pe):
            mm = nc.tensor.matmul
            tr = nc.tensor.transpose
            def attention_weights():
                pe.wait_ge(cst, 6)
                pe.wait_ge(w_at, 16 * N_AT)
                for j, (w, to) in enumerate(((wuq, bank[0]), (wuk, bank[0]), (wuv, bank[1]))):
                    for h in range(H):
                        c = (j % 2) * H * DC + h * DC
                        tr(to[:, c:c + DC], w[:, h * DK:(h + 1) * DK], ident[0:DC, 0:DC])
                for j in range(3):
                    c = H * DC + j * H
                    last = tr(bank[1][:, c:c + H], brow[:, j, :], ident[0:H, 0:H])
                last.then_inc(su_pe, 1)
                pe.wait_ge(su_dve, 2)
                for h in range(H):
                    last = mm(bank[2][0:KQ, h * (DC + 1):(h + 1) * (DC + 1)], LQ[:, h, :], RK[:, h, :],
                              start=True, stop=True)
                last.then_inc(su_pe, 1)
                for h in range(H):
                    r = (h % G) * DC
                    mm(bank[3][r:r + DC, (h // G) * D:(h // G + 1) * D], uvT[:, h, :], wo[:, h, :],
                       start=True, stop=True)
                for h in range(H):
                    last = mm(bank[4][:, 0:D], buvb[:, h, :], wo[:, h, :], start=(h == 0), stop=(h == H - 1))
                last.then_inc(su_pe, 1)
                pe.wait_ge(su_dve, 11)

            def ffn_weights():
                pe.wait_ge(w_ff, 16 * N_FF)
                pe.wait_ge(su_act, 2)
                mm(bank[5][:, 0:2], ones128, gsum, start=True, stop=True)
                tr(bank[5][:, NF:2 * NF], b1row, ident[0:NF, 0:NF]).then_inc(su_pe, 1)
                pe.wait_ge(mx_done, 6 * NT)
                pe.wait_ge(ga_free, len(TASKS_A) - 1)
                pe.wait_ge(qh_done, 2 * H)
                for i in range(8):
                    if i == 0:
                        pe.wait_ge(su_dve, 15)
                    if i == 4:
                        pe.wait_ge(su_dve, 17)
                    for j in range(4):
                        if i < 4:
                            src = w1n[:, (i % 2) * 4 + j, (i // 2) * P:(i // 2 + 1) * P]
                        else:
                            n = 2 * (i - 4) + j // 2
                            src = w2n[:, j % 2, n * P:(n + 1) * P]
                        last = tr(bank[i][:, j * P:(j + 1) * P], src, ident[:, :])
                    last.then_inc(su_pe, 1)
                pe.wait_ge(su_dve, 25)

            def step(st):
                s = st.s
                for h in range(SLOTS):
                    for t in range(SEGS):
                        tok = slice(t * P, (t + 1) * P)
                        if st.sm:
                            n = s * H * NT + h * NT + t
                            if (h, t) == (0, 0):
                                pe.wait_ge(ga_free, a_index(before(st), "R0") + 1)
                            if (h, t) == (G, 0):
                                pe.wait_ge(ga_free, a_index(st, "R1") + 1)
                            wait(pe, e_done, n - 1)
                            mm(ST[t % 2][:, :], KA[st.par][:, tok], QA[:, h, :], start=True, stop=False)
                            mm(ST[t % 2][:, :], KB[st.par][0:W + G, tok], QB[:, h, :], start=False,
                               stop=True).then_inc(st_full, 1)
                        task = TASKS_A.get((h, t), "")
                        if task and st.has_a(task):
                            pe_a_task(st, task, a_index(st, task))
                        if (h >= 2 and st.qk) or (h < 2 and st.sm):
                            b, head, p = (s + 1, h - 2, 1 - st.par) if h >= 2 else (s, h + 6, st.par)
                            if t == 0:
                                src = st if h >= 2 else before(st)
                                pe.wait_ge(ga_free, a_index(src, f"Q{head}") + 1)
                            wait(pe, mx_done, b * H * NT + head * NT + t - 1)
                            mm(MX[t % 2][:, :], QA[:, head, tok], KA[p][:, :], start=True, stop=True).then_inc(mx_full, 1)
                        task = TASKS_F.get((h, t), "")
                        if task and st.has_f(task):
                            pe_f_task(st, task, f_index(st, task))
                        if t == 1 and ((h < G and st.out) or (h >= G and st.sm)):
                            b, gr, p = (s - 1, 1, 1 - st.par) if h < G else (s, 0, st.par)
                            i = h % G
                            if i == 0:
                                pe.wait_ge(e_done, (b * H + (gr + 1) * G) * NT)
                                wait(pe, un_done, b * NG + gr)
                            for j in range(G):
                                r = slice(j * DC, (j + 1) * DC)
                                last = mm(U[r, :], V[p][:, i, :], E[:, gr * G + j, i, :], start=(i == 0),
                                          stop=(i == NT - 1))
                            last.then_inc(pv_full, 1)
                        if t == 2 and ((h == 0 and st.out) or (h == G and st.sm)):
                            b, gr = (s - 1, 1) if h == 0 else (s, 0)
                            pe.wait_ge(es_done, (b * H + (gr + 1) * G) * 3)
                            wait(pe, rec_done, (b * NG + gr) * 4)
                            for j in range(G):
                                r = slice(j * DC, (j + 1) * DC)
                                last = mm(L[r, :], ones32[:, :], esum[:, j, :], start=True, stop=True)
                            last.then_inc(l_full, 1)

            def pe_a_task(st, task, n):
                kind = task[0]
                b, p = st.s + 1, 1 - st.par
                wait(pe, ga_free, n)
                tasks = [t for t in TASKS_A.values() if st.has_a(t)]
                came = tasks[tasks.index(task) - 1]
                if task == tasks[0]:
                    wait(pe, qh_done, b * 2 * H)
                elif came[0] == "Q":
                    pe.wait_ge(qh_done, b * 2 * H + 2 * int(came[1]) + 2)
                if kind == "X":
                    if task == "X0":
                        pe.wait_ge(xln_done, b + 1)
                    for t in range(NT):
                        last = tr(GA[:, t * P:(t + 1) * P], xln[:, t, int(task[1]) * P:(int(task[1]) + 1) * P], ident[:, :])
                elif kind == "K":
                    for k in range(KD):
                        last = mm(GA[0:W + DC, :], wk[:, k, :], xT[:, k, :], start=(k == 0), stop=(k == KD - 1))
                elif kind == "Q":
                    if task == "Q0":
                        pe.wait_ge(c_done, 2 * b + 2)
                    last = mm(GA[:, :], AQ[:, int(task[1]), :, :].rearrange("k a c -> k (a c)"), cq[0:KQ, :], start=True, stop=True)
                elif kind == "S":
                    for t in range(NT):
                        last = mm(GA[:, t * H:(t + 1) * H], cq[0:KQ, t * P:(t + 1) * P], AC[:, :], start=True, stop=True)
                elif kind == "V":
                    for t in range(NT):
                        last = mm(GA[:, t * DC:(t + 1) * DC], kf[0:DC, t * P:(t + 1) * P], ident[0:DC, 0:DC],
                                  start=True, stop=True)
                elif kind == "R":
                    gr = int(task[1])
                    pe.wait_ge(sh_done, (st.s if gr else b) * NG + gr + 1)
                    for t in range(NT):
                        last = mm(GA[0:W + G, t * P:(t + 1) * P], shift[:, t, :], identr[:, :], start=True, stop=True)
                last.then_inc(ga_full, 1)

            def pe_f_task(st, task, n):
                kind = task[0]
                wait(pe, gf_free, n)
                i = int(task[1])
                if kind == "O":
                    if i == 0:
                        pe.wait_ge(un_done, st.s * NG)
                    for t in range(2):
                        q = slice((2 * i + t) * P, (2 * i + t + 1) * P)
                        for gr in range(NG):
                            last = mm(GF[:, t * D:(t + 1) * D], un[:, gr, q], M[:, gr, :], start=(gr == 0), stop=(gr == NG - 1))
                elif kind == "T":
                    if i == 0:
                        pe.wait_ge(yln_done, st.s)
                    for t in range(NT):
                        last = tr(GF[:, t * P:(t + 1) * P], yln[:, t, i * P:(i + 1) * P], ident[:, :])
                elif kind == "H":
                    f = slice(i * P, (i + 1) * P)
                    for k in range(KD):
                        mm(GF[:, :], w1T[:, k, f], yh[:, k, :], start=(k == 0), stop=False)
                        last = mm(GF[:, :], w1T[:, k, f], yl[:, k, :], start=False, stop=(k == KD - 1))
                elif kind == "Y":
                    q = slice(i * P, (i + 1) * P)
                    if i == 0:
                        pe.wait_ge(hl_done, (st.s - 1) * NF)
                    for f in range(NF):
                        mm(GF[:, 0:D], hh[:, f, q], w2T[:, f, :], start=(f == 0), stop=False)
                        last = mm(GF[:, 0:D], hl[:, f, q], w2T[:, f, :], start=False, stop=(f == NF - 1))
                last.then_inc(gf_full, 1)

            steps(pe, step, attention_weights, ffn_weights)


_INS = ["L0_attn_h_t", "L0_attn_W_DQ", "L0_attn_b_DQ", "L0_attn_W_UQ", "L0_attn_b_UQ", "L0_attn_W_DKV",
        "L0_attn_b_DKV", "L0_attn_W_UK", "L0_attn_b_UK", "L0_attn_W_UV", "L0_attn_b_UV", "L0_attn_W_QR",
        "L0_attn_b_QR", "L0_attn_W_KR", "L0_attn_b_KR", "L0_attn_W_O", "L0_attn_b_O", "L0_ffn_W1", "L0_ffn_b1",
        "L0_ffn_W2", "L0_ffn_b2"]


def kernel(**inputs):
    import numpy as _np
    import concourse.bacc as _bacc
    from concourse import mybir as _mybir
    from concourse.bass_utils import run_bass_kernel_spmd as _run

    nc = _bacc.Bacc("TRN2", target_bir_lowering=False, num_devices=1)
    arrays, args = {}, []
    for name in _INS:
        a = _np.ascontiguousarray(inputs[name])
        arrays[f"in_{name}"] = a
        args.append(nc.dram_tensor(f"in_{name}", a.shape, _mybir.dt.from_np(a.dtype), kind="ExternalInput").ap())
    shape = inputs["L0_attn_h_t"].shape
    args.append(nc.dram_tensor("out_0", shape, F32, kind="ExternalOutput").ap())
    layer_kernel(nc, *args)
    r = _run(nc, [arrays], core_ids=[0])
    return r.results[0]["out_0"]
```

```python
from contextlib import ExitStack

import concourse.bass as bass
from concourse import mybir

F32 = mybir.dt.float32
F32R = mybir.dt.float32r
ALU = mybir.AluOpType
ACT = mybir.ActivationFunctionType
AX = mybir.AxisListType

P = 128
SLOTS, SEGS = 8, 4

TASKS_A = {(0, 1): "X0", (0, 2): "X1", (0, 3): "K", (1, 2): "Q0", (2, 0): "S", (2, 1): "Q1", (2, 3): "R1",
           (3, 1): "Q2", (4, 1): "Q3", (5, 0): "Q4", (5, 3): "V", (6, 1): "Q5", (6, 3): "R0", (7, 1): "Q6",
           (7, 3): "Q7"}
TASKS_F = {(0, 0): "H0", (0, 2): "H1", (1, 0): "H2", (1, 2): "H3", (2, 0): "H4", (2, 2): "H5", (3, 0): "H6",
           (3, 2): "H7", (4, 0): "O0", (4, 2): "O1", (5, 0): "Y0", (5, 2): "Y1", (6, 0): "Y2", (6, 2): "T0",
           (7, 0): "T1", (7, 2): "Y3"}

RECIPROCALS = {(2, 0): (1, 0), (2, 1): (1, 1), (2, 2): (1, 2), (2, 3): (1, 3), (6, 1): (0, 0), (6, 3): (0, 1),
               (7, 0): (0, 2), (7, 2): (0, 3)}
LAST_RECIPROCALS = {(0, 2): (1, 0), (0, 3): (1, 1), (1, 0): (1, 2), (1, 1): (1, 3)}
AT = {"ln stats": (4, 1), "ln pow": (4, 0), "ln norm": (5, 3),
      "ln2 stats": (5, 1), "ln2 pow": (5, 2), "ln2 norm": (6, 0),
      "split K": (1, 0),
      "shift 0": (6, 0), "shift 1": (1, 3),
      "sums 0": (4, 3), "sums 1": (0, 1),
      "norm 0": (7, 3), "norm 1": (3, 0),
      "add b_attn": (0, 0), "add b2": (6, 2)}

LAG = {"S": 0, "Q0": 1, "Q1": 1, "Q2": 2, "Q3": 1, "Q4": 1, "Q5": 0, "Q6": 2, "Q7": 2, "H0": 4, "H1": 2, "H2": 1,
       "H3": 5, "H4": 3, "H5": 2, "H6": 1, "H7": 3, "O0": 1, "O1": 2, "Y0": 2, "Y1": 2, "Y2": 1, "Y3": 1, "T0": 1,
       "T1": 1}


def lagged(tasks):
    places = {}
    for (h, t), task in sorted(tasks.items()):
        if task in LAG:
            n = min(2 * (h * SEGS + t) + LAG[task], 2 * SLOTS * SEGS - 1)
            places.setdefault((n // 2 // SEGS, n // 2 % SEGS, n % 2), []).append(task)
    return places


class Step:

    def __init__(self, s, nb, parity=None):
        self.s, self.full = s, parity is not None
        self.par = parity if self.full else s % 2
        live = lambda b: self.full or 0 <= b < nb
        self.ln, self.qk, self.sm, self.out, self.ffn = (live(s + d) for d in ((2, 1, 0, -1, -2)))

    def has_a(self, task):
        return self.sm if task == "R1" else self.qk

    def has_f(self, task):
        return self.ffn if task[0] in "HY" else self.out


def layer_kernel(nc, x, W_DQ, b_DQ, W_UQ, b_UQ, W_DKV, b_DKV, W_UK, b_UK, W_UV, b_UV, W_QR, b_QR, W_KR, b_KR,
                 W_O, b_O, W1, b1, W2, b2, out):
    NB, S, D = x.shape
    DC = W_DQ.shape[1]
    DR = W_KR.shape[1]
    H = W_QR.shape[1] // DR
    DK = W_UQ.shape[1] // H
    F = W1.shape[0]
    KD = D // P
    NF = F // P
    NT = S // P
    W = DC + DR
    G = 4
    NG = H // G
    KQ = 3 * DC + 2
    SCALE = float(DK + DR) ** -0.5
    MAGIC = 1.5 * 2.0 ** 23
    EPS = 1e-5
    assert (S, D, DC, DR, DK, H) == (512, 256, 32, 32, 128, SLOTS) and NT == SEGS and F == 1024 and NB % 2 == 0

    ctx = ExitStack()
    with ctx:
        def sb(name, shape, dt=F32):
            return ctx.enter_context(nc.sbuf_tensor(name, shape, dt))

        def sem(name):
            return ctx.enter_context(nc.semaphore(name))

        bank = [ctx.enter_context(nc.psum_tensor(n, [P, 512], F32))
                for n in ("bST0", "bST1", "bMX0", "bMX1", "bU", "bL", "bGA", "bGF")]
        ST, MX, U, L, GA, GF = bank[0:2], bank[2:4], bank[4], bank[5], bank[6], bank[7]

        ident = sb("ident", [P, P])
        identr = sb("identr", [P, P], F32R)
        ones32 = sb("ones32", [P, 32])
        neghalf = sb("neghalf", [P, NT])
        headmask = sb("headmask", [P, G])
        wk = sb("wk", [P, KD, W + DC])
        bk = sb("bk", [P, 1])
        bc = sb("bc", [3 * DC, 1])
        AQ = sb("AQ", [KQ, H, 2, W], F32R)
        AC = sb("AC", [KQ, H], F32R)
        M = sb("M", [P, NG, D])
        battn = sb("battn", [P, D])
        b2row = sb("b2row", [P, D])
        b1col = sb("b1col", [P, NF])
        w1T = sb("w1T", [P, KD, F], F32R)
        w2T = sb("w2T", [P, NF, D], F32R)
        xln = sb("xln", [P, NT, D])
        xT = sb("xT", [P, KD, S])
        yln = xT[:, :, :].rearrange("p k s -> p (k s)").rearrange("p (t d) -> p t d", t=NT)
        kf = sb("kf", [P, S])
        cq = sb("cq", [P, S], F32R)
        KA = [sb(f"KA{i}", [P, S], F32R) for i in range(2)]
        KB = [sb(f"KB{i}", [P, S], F32R) for i in range(2)]
        V = [sb(f"V{i}", [P, NT, DC]) for i in range(2)]
        QA = sb("QA", [P, H, S], F32R)
        QB = sb("QB", [W + G, H, S], F32R)
        rowmax = sb("rowmax", [P, H, NT])
        const = [sb(f"const{i}", [P, NT, H]) for i in range(2)]
        mfull = sb("mfull", [P, G, NT])
        shift = sb("shift", [P, NT, W + G], F32R)
        E = sb("E", [P, H, NT, S])
        esum = sb("esum", [P, G, S])
        un = sb("un", [P, NG, S])
        x2 = [sb(f"x2_{i}", [P, NT, D]) for i in range(2)]
        stats = sb("stats", [P, NT, 6])
        mv = sb("mv", [P, 2, NT, 2])
        carrier = sb("carrier", [1, 2])
        vareps = sb("vareps", [P, 2, NT])
        rstd = sb("rstd", [P, 2, NT])
        yh = sb("yh", [P, KD, S], F32R)
        yl = sb("yl", [P, KD, S], F32R)
        hh = sb("hh", [P, NF, S], F32R)
        hl = sb("hl", [P, NF, S], F32R)
        ob = sb("ob", [P, 2, D])
        hf = ob[:, :, :].rearrange("p a d -> p (a d)")
        cf = un[0:3 * DC, 1, :]

        Ef = E[:, :, :, :].rearrange("p h t s -> p (h t s)")
        w1n = Ef[:, 0:2048].rearrange("p (n d) -> p n d", n=NF)
        w2n = Ef[:, 2048:4096].rearrange("p (n f) -> p n f", n=KD)
        wo = Ef[:, 4096:6144].rearrange("p (h n) -> p h n", h=H)
        wuq = Ef[0:DC, 6144:7168]
        wuk = Ef[0:DC, 7168:8192]
        wuv = Ef[0:DC, 8192:9216]
        LQ = Ef[:, 9216:9216 + H * KQ].rearrange("p (h c) -> p h c", h=H)
        RK = Ef[:, 10240:10240 + H * (DC + 1)].rearrange("p (h c) -> p h c", h=H)
        uvT = Ef[:, 10624:10880].rearrange("p (h c) -> p h c", h=H)
        buv = Ef[:, 11008:11264].rearrange("p (h c) -> p h c", h=H)
        bsum = Ef[:, 11264:11264 + D]
        AF = Ef[0:KQ, 12032:12032 + H * (W + 1)].rearrange("p (h c) -> p h c", h=H)
        alr = Ef[0:KQ, 12608:12608 + H * (W + 1)].rearrange("p (h c) -> p h c", h=H)
        brow = Ef[0:H, 15910:15910 + 3 * P].rearrange("h (k p) -> h k p", k=3)
        b1row = Ef[0:H, 13696:13696 + P]
        ones128 = Ef[:, 13312:13440]
        bot = Ef[:, 13440:13696]
        wabs = Ef[:, 13824:15872]
        gsum = Ef[:, 15900:15902]
        gcol = Ef[:, 15902:15904]
        grec = Ef[:, 15904:15906]
        negmagic = Ef[:, 15906:15907]
        tq = bank[0][:, 0:H * DC].rearrange("p (h c) -> p h c", h=H)
        tk = bank[1][:, 0:H * DC].rearrange("p (h c) -> p h c", h=H)
        tb = [bank[j][:, H * DC:H * DC + H] for j in range(2)]
        tv = L[:, 0:H * DC].rearrange("p (h c) -> p h c", h=H)
        tbv = L[:, H * DC:H * DC + H]
        TURN = (U, GF, ST[1], ST[0])
        w_qk = sem("w_qk")
        w_qr = sem("w_qr")
        w_x = sem("w_x")
        w_o = sem("w_o")
        w_f1 = sem("w_f1")
        w_f2 = sem("w_f2")
        cst = sem("cst")
        su_pe = sem("su_pe")
        su_dve = sem("su_dve")
        su_act = sem("su_act")
        row_sent = sem("row_sent")
        x_in = sem("x_in")
        xln_done = sem("xln_done")
        ga_full = sem("ga_full")
        ga_free = sem("ga_free")
        gf_full = sem("gf_full")
        gf_free = sem("gf_free")
        cf_done = sem("cf_done")
        k_done = sem("k_done")
        c_done = sem("c_done")
        qh_done = sem("qh_done")
        mx_full = sem("mx_full")
        mx_done = sem("mx_done")
        mf_done = sem("mf_done")
        sh_done = sem("sh_done")
        st_full = sem("st_full")
        e_done = sem("e_done")
        es_done = sem("es_done")
        pv_full = sem("pv_full")
        l_full = sem("l_full")
        rec_done = sem("rec_done")
        un_done = sem("un_done")
        xr_in = sem("xr_in")
        xb_done = sem("xb_done")
        st_done = sem("st_done")
        st2_done = sem("st2_done")
        mv_done = sem("mv_done")
        mv2_done = sem("mv2_done")
        ve_done = sem("ve_done")
        ve2_done = sem("ve2_done")
        rs_done = sem("rs_done")
        rs2_done = sem("rs2_done")
        yln_done = sem("yln_done")
        x2b_done = sem("x2b_done")
        yh_done = sem("yh_done")
        hh_done = sem("hh_done")
        hl_done = sem("hl_done")
        o_sent = [sem(f"o_sent{i}") for i in range(2)]

        def wait(eng, s, value):
            if isinstance(value, int) and value <= 0:
                return
            eng.wait_ge(s, value)

        N_QK, N_QR, N_X, N_F2, N_O = 4, 5, 10, 3, 4

        def a_index(st, task):
            mine = [t for t in TASKS_A.values() if st.has_a(t)].index(task)
            return mine if not st.full and st.s == -1 else st.s * len(TASKS_A) + (len(TASKS_A) - 1) + mine

        def f_index(st, task):
            mine = [t for t in TASKS_F.values() if st.has_f(t)].index(task)
            return mine if not st.full and st.s == 1 else (st.s - 2) * len(TASKS_F) + 4 + mine

        def before(st):
            return Step(st.s - 1, NB, 1 - st.par) if st.full else Step(st.s - 1, NB)

        def f_after_prev(st, task):
            if st.full:
                mine = list(TASKS_F.values()).index(task)
                return (st.s - 3) * len(TASKS_F) + 4 + mine + 1
            p = Step(st.s - 1, NB)
            return f_index(p, task) + 1 if p.has_f(task) else 0

        def f_bank(st, n):
            return GF if st.full or st.sm or n % 2 == 0 else GA

        def f_freed(st, task, n):
            if not (st.full or st.sm):
                tasks = [t for t in TASKS_F.values() if st.has_f(t)]
                i = tasks.index(task)
                if i >= 2 and tasks[i - 1][0] == tasks[i - 2][0]:
                    return n - 1
            return n

        def hidden_order(st):
            return (0, 0, 1, 2, 0, 1, 2, 0) if st.full or st.qk else (1, 2, 0, 1, 2, 0, 1, 2)

        def hidden(st, f):
            return (hf, xT[:, 0, :], xT[:, 1, :])[hidden_order(st)[f]]

        def hidden_before(st, f):
            order = hidden_order(st)
            return max([g + 1 for g in range(f) if order[g] == order[f]], default=0)

        def steps(eng, body, q_weights=None):
            body(Step(-2, NB))
            if q_weights:
                q_weights()
            body(Step(-1, NB))
            body(Step(0, NB))
            body(Step(1, NB))
            with eng.Fori(1, NB // 2 - 1) as pair:
                body(Step(pair * 2, NB, 0))
                body(Step(pair * 2 + 1, NB, 1))
            for s in range(NB - 2, NB + 2):
                body(Step(s, NB))

        block = ctx.enter_context(nc.Block())

        @block.sync
        def _(sp):
            def loads(arrived):
                def at(dst, src):
                    with nc.allow_non_contiguous_dma(reason="short bias columns, once"):
                        sp.dma_start(dst, src).then_inc(arrived, 16)
                return at
            sp.dma_start(xln[:, :, :], x[0].rearrange("(t p) d -> p t d", p=P)).then_inc(x_in, 16)
            at = loads(w_qk)
            at(wuq, W_UQ)
            at(wuk, W_UK)
            for j, b in enumerate((b_UQ, b_UK)):
                at(brow[:, j, :], b.rearrange("(h p) -> h p", p=P))
            at = loads(w_qr)
            for j in range(3):
                at(AF[j * DC:(j + 1) * DC, :, DC:W], W_QR.rearrange("c (h r) -> c h r", h=H))
            for j in range(2):
                at(AF[3 * DC + j:3 * DC + j + 1, :, DC:W], b_QR.rearrange("(a h r) -> a h r", a=1, h=H))
            at = loads(w_f1)
            at(w1n, W1.rearrange("(n p) d -> p n d", p=P))
            at = loads(w_x)
            for j, w in enumerate((W_DKV, W_KR, W_DQ)):
                at(wk[:, :, j * DC:(j + 1) * DC], w.rearrange("(k p) c -> p k c", p=P))
            for j in range(2):
                at(bk[j * W:j * W + DC, :], b_DKV.rearrange("(c a) -> c a", a=1))
                at(bk[j * W + DC:(j + 1) * W, :], b_KR.rearrange("(c a) -> c a", a=1))
            for j in range(3):
                at(bc[j * DC:(j + 1) * DC, :], b_DQ.rearrange("(c a) -> c a", a=1))
            sp.wait_ge(su_dve, 9)
            sp.dma_start(AQ[KQ - 1:KQ, :, 0, :].bitcast(F32), alr[KQ - 1:KQ, :, 0:W]).then_inc(row_sent, 16)
            with nc.allow_non_contiguous_dma(reason="eight numbers"):
                sp.dma_start(AC[KQ - 1:KQ, :].bitcast(F32), alr[KQ - 1:KQ, :, W]).then_inc(row_sent, 16)

            at = loads(w_f2)
            at(w2n, W2.rearrange("(n p) f -> p n f", p=P))
            at(b1row, b1.rearrange("(n p) -> n p", p=P))
            at(b2row[:, :], b2.rearrange("(a n) -> a n", a=1).broadcast_to([P, D]))
            at = loads(w_o)
            at(wuv, W_UV)
            at(brow[:, 2, :], b_UV.rearrange("(h p) -> h p", p=P))
            at(wo, W_O.rearrange("(h p) n -> p h n", p=P))
            at(bot, b_O.rearrange("(a n) -> a n", a=1).broadcast_to([P, D]))

            def step(st):
                s = st.s
                if st.out:
                    wait(sp, gf_free, f_after_prev(st, "Y3"))
                    b = s - 1
                    sp.dma_start(x2[1 - st.par][:, :, :],
                                 x[bass.ds(b, 1)].rearrange("a (t p) d -> p (a t) d", p=P)).then_inc(xr_in, 16)
                if st.ln and not (not st.full and s == -2):
                    wait(sp, ga_full, a_index(st, "X1") + 1)
                    sp.dma_start(xln[:, :, :],
                                 x[bass.ds(s + 2, 1)].rearrange("a (t p) d -> p (a t) d", p=P)).then_inc(x_in, 16)
                if st.ffn:
                    for t in range(NT):
                        sp.wait_ge(gf_free, f_index(st, f"Y{t}") + 1)
                        sp.dma_start(out[bass.ds(s - 2, 1), t * P:(t + 1) * P, :].rearrange("a p d -> p (a d)"),
                                     ob[:, t % 2, :]).then_inc(o_sent[t % 2], 16)
            steps(sp, step)
            for i in range(2):
                sp.wait_ge(o_sent[i], 8 * NB * NT + 16)

        @block.gpsimd
        def _(pool):
            g = nc.gpsimd
            g.memset(ident[:, :], 0.0).then_inc(cst, 1)
            g.memset(headmask[:, :], 0.0).then_inc(cst, 1)
            pool.wait_ge(cst, 2)
            g.affine_select(out=ident[:, :], in_=ident[:, :], compare_op=ALU.not_equal, fill=1.0, base=0,
                            pattern=[[-1, P]], channel_multiplier=1).then_inc(cst, 1)
            g.affine_select(out=headmask[:, :], in_=headmask[:, :], compare_op=ALU.not_equal, fill=1.0, base=-W,
                            pattern=[[-1, G]], channel_multiplier=1).then_inc(cst, 1)
            g.memset(ones32[:, :], 1.0).then_inc(o_sent[0], 16)
            g.memset(neghalf[:, :], -0.5).then_inc(o_sent[1], 16)
            g.memset(ones128, 1.0).then_inc(cst, 1)
            g.memset(negmagic, -MAGIC).then_inc(cst, 1)
            g.memset(shift[:, :, :].bitcast(F32), 0.0).then_inc(cst, 1)
            pool.wait_ge(cst, 7)

            def step(st):
                s = st.s
                for h in range(SLOTS):
                    for t in range(SEGS):
                        if st.out and (h, t) == AT["add b_attn"]:
                            pool.wait_ge(xr_in, s * 16)
                            g.tensor_tensor(x2[1 - st.par][:, :, :], x2[1 - st.par][:, :, :],
                                            battn[:, None, :].broadcast_to([P, NT, D]), ALU.add).then_inc(xb_done, 1)
                        if st.ln and (h, t) == AT["ln pow"]:
                            pool.wait_ge(ve_done, s + 3)
                            g.tensor_tensor(rstd[:, 0, :], vareps[:, 0, :], neghalf[:, :], ALU.pow).then_inc(rs_done, 1)
                        if st.out and (h, t) == AT["ln2 pow"]:
                            pool.wait_ge(ve2_done, s)
                            g.tensor_tensor(rstd[:, 1, :], vareps[:, 1, :], neghalf[:, :], ALU.pow).then_inc(rs2_done, 1)
                        if st.out and (h, t) == AT["add b2"]:
                            pool.wait_ge(yln_done, s)
                            g.tensor_tensor(x2[1 - st.par][:, :, :], x2[1 - st.par][:, :, :],
                                            b2row[:, None, :].broadcast_to([P, NT, D]), ALU.add).then_inc(x2b_done, 1)
                        if st.sm and t >= 1:
                            pool.wait_ge(e_done, s * H * NT + h * NT + t + 1)
                            if t == 1 and h % G == 0:
                                wait(pool, l_full, s * NG + h // G)
                            if t > 1:
                                pool.wait_ge(es_done, s * 3 * H + 3 * h + t - 1)
                            first = E[:, h, 0, :] if t == 1 else esum[:, h % G, :]
                            g.tensor_tensor(esum[:, h % G, :], first, E[:, h, t, :], ALU.add).then_inc(es_done, 1)
                        task = TASKS_F.get((h, t), "")
                        if st.ffn and st.sm and task.startswith("H"):
                            f = int(task[1])
                            pool.wait_ge(hh_done, (s - 2) * NF + f + 1)
                            g.tensor_tensor(hl[:, f, :], hidden(st, f), hh[:, f, :], ALU.subtract).then_inc(hl_done, 1)
            steps(pool, step)

        @block.scalar
        def _(act):
            a = nc.scalar
            def abs_sum(j):
                act.wait_ge((w_f1, w_f2)[j], 16 * (1, N_F2)[j])
                act.wait_ge(su_act, j + 1)
                a.activation(wabs, Ef[:, 2048 * j:2048 * (j + 1)], ACT.Abs,
                             accum_out=gsum[:, j:j + 1]).then_inc(su_act, 1)

            def q_weights():
                act.wait_ge(su_pe, 1)
                a.activation(RK[:, :, 0:DC], tk, ACT.Copy)
                a.activation(RK[:, :, DC], tb[1], ACT.Copy).then_inc(su_act, 1)
                abs_sum(0)

            def other_weights(h):
                if h == 1:
                    abs_sum(1)
                if h == 2:
                    act.wait_ge(su_pe, 3)
                    a.activation(uvT, tv, ACT.Copy)
                    a.activation(buv, tbv[:, :, None].broadcast_to([P, H, DC]), ACT.Copy).then_inc(su_act, 1)
                if h == 4:
                    act.wait_ge(su_pe, 5)
                    a.activation(M[:, :, :].rearrange("p g d -> p (g d)"), ST[0][:, :], ACT.Copy)
                    a.activation(bsum, ST[1][:, 0:D], ACT.Copy, scale=1.0 / DC).then_inc(su_act, 1)
                if h in (5, 6):
                    for i in range(4 * (h - 5), 4 * (h - 4)):
                        act.wait_ge(su_pe, 6 + i if i < 4 else 7 + i)
                        if i < 4:
                            dst = w1T[:, i // 2, (i % 2) * 512:(i % 2 + 1) * 512]
                        else:
                            dst = w2T[:, 2 * (i - 4):2 * (i - 4) + 2, :].rearrange("p n d -> p (n d)")
                        a.activation(dst, TURN[i % 4][:, :], ACT.Identity, bias=negmagic).then_inc(su_act, 1)

            def step(st):
                s = st.s
                for h in range(SLOTS):
                    for t in range(SEGS):
                        if st.sm:
                            n = s * H * NT + h * NT + t
                            if t == 0:
                                wait(act, pv_full, (s - 1) * NG * NT + (h // G + 1) * NT)
                                wait(act, es_done, (s - 1) * 3 * H + 3 * h + 3)
                            act.wait_ge(st_full, n + 1)
                            a.activation(E[:, h, t, :], ST[t % 2][:, :], ACT.Exp, scale=SCALE).then_inc(e_done, 1)
                        task = TASKS_A.get((h, t), "")
                        if task and st.has_a(task):
                            n = a_index(st, task)
                            act_a_task(st, task, n)
                        task = TASKS_F.get((h, t), "")
                        if task and st.has_f(task):
                            act_f_task(st, task, f_index(st, task))
                    if not st.full and s == -1:
                        other_weights(h)

            def act_a_task(st, task, n):
                kind = task[0]
                b = st.s + 1
                if kind in "XKVR":
                    act.wait_ge(ga_full, n + 1)
                if kind == "X":
                    a.activation(xT[:, int(task[1]), :], GA[:, :], ACT.Copy).then_inc(ga_free, 1)
                elif kind == "K":
                    wait(act, c_done, 2 * b)
                    for j in range(3):
                        q = slice(j * DC, (j + 1) * DC)
                        last = a.activation(cf[q, :], GA[W:W + DC, :], ACT.Identity, bias=bc[q, 0:1])
                    last.then_inc(cf_done, 1)
                    wait(act, k_done, 2 * b)
                    for j in range(2):
                        q = slice(j * W, (j + 1) * W)
                        last = a.activation(kf[q, :], GA[0:W, :], ACT.Identity, bias=bk[q, 0:1])
                    last.then_inc(ga_free, 1)
                elif kind == "V":
                    wait(act, pv_full, (st.s) * NG * NT)
                    a.activation(V[1 - st.par][:, :, :],
                                 GA[:, :].rearrange("p (t c) -> p t c", t=NT)[:, :, 0:DC], ACT.Copy).then_inc(ga_free, 1)
                elif kind == "R":
                    gr = int(task[1])
                    if gr == 1:
                        wait(act, st_full, st.s * H * NT)
                    else:
                        wait(act, st_full, st.s * H * NT + G * NT if st.sm else 0)
                    for j in range(G):
                        last = a.activation(QB[W:W + G, gr * G + j, :], GA[W:W + G, :], ACT.Copy,
                                            scale=headmask[W:W + G, j:j + 1])
                    last.then_inc(ga_free, 1)
                elif kind == "Q":
                    h = int(task[1])
                    act.wait_ge(ga_full, n + 1)
                    if st.sm:
                        wait(act, st_full, st.s * H * NT + (h + 1) * NT)
                        wait(act, mx_full, st.s * H * NT + (h + 1) * NT)
                    a.activation(QA[:, h, :], GA[:, :], ACT.Copy).then_inc(qh_done, 1)
                    a.activation(QB[0:W, h, :], GA[0:W, :], ACT.Copy).then_inc(qh_done, 1)

            def act_f_task(st, task, n):
                kind, fbank = task[0], f_bank(st, n)
                if kind == "T":
                    act.wait_ge(gf_full, n + 1)
                    a.activation(yh[:, int(task[1]), :], fbank[:, :], ACT.Copy).then_inc(yh_done, 1)
                elif kind == "H":
                    f = int(task[1])
                    act.wait_ge(gf_full, n + 1)
                    if hidden_before(st, f):
                        act.wait_ge(hl_done, (st.s - 2) * NF + hidden_before(st, f))
                    if f == hidden_order(st).index(0):
                        for i in range(2):
                            act.wait_ge(o_sent[i], 8 * NT * (st.s - 2) + 16)
                    a.activation(hidden(st, f), fbank[:, :], ACT.Relu, bias=b1col[:, f:f + 1]).then_inc(gf_free, 1)

            steps(act, step, q_weights)

        @block.vector
        def _(dve):
            v = nc.vector
            LAGGED_A, LAGGED_F = lagged(TASKS_A), lagged(TASKS_F)
            done = [0]

            def su(ins):
                done[0] += 1
                ins.then_inc(su_dve, 1)
            v.memset(cq[3 * DC:KQ, :].bitcast(F32), 1.0)
            for i in range(2):
                v.memset(KB[i][W:W + G, :].bitcast(F32), 1.0)
            def q_weights():
                dve.wait_ge(cst, 7)
                su(v.tensor_copy(identr[:, :], ident[:, :]))
                dve.wait_ge(su_pe, 1)
                for j in range(3):
                    v.tensor_copy(LQ[:, :, j * DC:(j + 1) * DC], tq)
                for j in range(2):
                    last = v.tensor_copy(LQ[:, :, 3 * DC + j], tb[0])
                su(last)
                dve.wait_ge(w_qr, 16 * N_QR)
                dve.wait_ge(su_pe, 2)
                prod = bank[2][0:KQ, 0:H * (DC + 1)].rearrange("p (h c) -> p h c", h=H)
                su(v.tensor_copy(AF[:, :, 0:DC], prod[:, :, 0:DC]))
                su(v.tensor_copy(AF[:, :, W], prod[:, :, DC]))
                dve.wait_ge(su_dve, 4)
                su(v.tensor_copy(AQ[:, :, 0, :], AF[:, :, 0:W]))
                su(v.tensor_copy(AC[:, :], AF[:, :, W]))
                dve.wait_ge(su_dve, 6)
                v.tensor_tensor(alr[:, :, 0:W], AF[:, :, 0:W], AQ[:, :, 0, :], ALU.subtract)
                su(v.tensor_tensor(alr[:, :, W], AF[:, :, W], AC[:, :], ALU.subtract))
                dve.wait_ge(su_dve, 7)
                lo = slice(2 * DC, 3 * DC)
                su(v.tensor_copy(AQ[lo, :, 0, :], alr[lo, :, 0:W]))
                su(v.tensor_copy(AC[lo, :], alr[lo, :, W]))
                dve.wait_ge(row_sent, 32)
                su(v.tensor_copy(AQ[:, :, 1, :], AQ[:, :, 0, :]))

            def clip(j):
                wj = Ef[:, 2048 * j:2048 * (j + 1)]
                su(v.tensor_scalar(wj, wj, grec[:, j:j + 1], -1.0, ALU.mult, ALU.max))
                dve.wait_ge(su_dve, done[0])
                su(v.tensor_scalar(wj, wj, 1.0, MAGIC, ALU.min, ALU.add))

            def other_weights(h):
                if h == 3:
                    dve.wait_ge(su_pe, 4)
                    v.tensor_copy(b1col[:, :], GF[:, NF:2 * NF])
                    su(v.tensor_scalar(gcol, GF[:, 0:2], 1.0 / (F * D), EPS, ALU.mult, ALU.add))
                    dve.wait_ge(su_dve, 11)
                    su(v.reciprocal(grec, gcol))
                    dve.wait_ge(su_dve, 12)
                    clip(0)
                if h == 4:
                    clip(1)
                if h == 6:
                    dve.wait_ge(su_pe, 10)
                    su(v.tensor_tensor(battn[:, :], L[:, 0:D], bot, ALU.add))

            def shift_group(b, par, gr, before_full):
                dve.wait_ge(mx_done, b * H * NT + (gr + 1) * G * NT)
                wait(dve, mf_done, b * NG + gr)
                c = const[par][:, :, gr * G:(gr + 1) * G].rearrange("p t h -> p h t")
                v.tensor_tensor(mfull[:, :, :], rowmax[:, gr * G:(gr + 1) * G, :], c, ALU.add).then_inc(mf_done, 1)
                dve.wait_ge(mf_done, b * NG + gr + 1)
                wait(dve, ga_full, before_full)
                v.tensor_tensor(shift[:, :, W:W + G].rearrange("p t h -> p h t"), c, mfull[:, :, :],
                                ALU.subtract).then_inc(sh_done, 1)

            def ln_stats(src, which, ready, made, mvd, ved, b):
                ready()
                for t in range(NT):
                    last = v.bn_stats(stats[:, t, :], src[:, t, :])
                last.then_inc(made, 1)
                dve.wait_ge(made, b + 1)
                v.memset(carrier[0:1, which:which + 1], 0.0)
                for t in range(NT):
                    last = v.bn_aggr(mv[:, which, t, :], stats[:, t, :])
                last.then_inc(mvd, 1)
                dve.wait_ge(mvd, b + 1)
                v.tensor_scalar(vareps[:, which, :], mv[:, which, :, 1], EPS, None, ALU.add).then_inc(ved, 1)

            def step(st):
                s = st.s
                for h in range(SLOTS):
                    for t in range(SEGS):
                        for task in LAGGED_A.get((h, t, 0), ()):
                            if st.has_a(task):
                                dve_a_task(st, task, a_index(st, task))
                        for task in LAGGED_F.get((h, t, 0), ()):
                            if st.has_f(task):
                                dve_f_task(st, task, f_index(st, task))
                        if (h >= 2 and st.qk) or (h < 2 and st.sm):
                            b, head = (s + 1, h - 2) if h >= 2 else (s, h + 6)
                            if t == 0:
                                wait(dve, mf_done, (b - 1) * NG + head // G + 1)
                            dve.wait_ge(mx_full, b * H * NT + head * NT + t + 1)
                            v.reduce_max(rowmax[:, head, t:t + 1], MX[t % 2][:, :], AX.X).then_inc(mx_done, 1)
                        if st.qk and (h, t) == AT["split K"]:
                            dve_a_task(st, "K", a_index(st, "K"))
                        if st.sm and (h, t) == AT["shift 1"]:
                            shift_group(s, st.par, 1, a_index(before(st), "R0") + 1)
                        if st.qk and (h, t) == AT["shift 0"]:
                            shift_group(s + 1, 1 - st.par, 0, a_index(st, "R1") + 1 if st.sm else 0)
                        for task in LAGGED_A.get((h, t, 1), ()):
                            if st.has_a(task):
                                dve_a_task(st, task, a_index(st, task))
                        for task in LAGGED_F.get((h, t, 1), ()):
                            if st.has_f(task):
                                dve_f_task(st, task, f_index(st, task))
                        places = RECIPROCALS if st.full or st.sm else LAST_RECIPROCALS
                        gr, i = places.get((h, t), (None, 0))
                        if (gr == 1 and st.out) or (gr == 0 and st.sm):
                            b = s - gr
                            dve.wait_ge(l_full, b * NG + gr + 1)
                            c = slice(i * P, (i + 1) * P)
                            if i == 0 and gr == 0:
                                wait(dve, gf_full, f_index(st, "O1") + 1 if st.out else 0)
                            if i == 0 and gr == 1 and st.qk:
                                dve.wait_ge(c_done, 2 * (s + 1) + 2)
                            v.reciprocal(un[:, gr, c], L[:, c]).then_inc(rec_done, 1)
                        if ((h, t) == AT["norm 1"] and st.out) or ((h, t) == AT["norm 0"] and st.sm):
                            b, gr = (s - 1, 1) if (h, t) == AT["norm 1"] else (s, 0)
                            dve.wait_ge(pv_full, (b * NG + gr + 1) * NT)
                            dve.wait_ge(rec_done, (b * NG + gr + 1) * 4)
                            v.tensor_tensor(un[:, gr, :], U[:, :], un[:, gr, :], ALU.mult).then_inc(un_done, 1)
                        if st.ln and (h, t) == AT["ln stats"]:
                            ln_stats(xln, 0, lambda: dve.wait_ge(x_in, (s + 3) * 16), st_done, mv_done, ve_done, s + 2)
                        if st.ln and (h, t) == AT["ln norm"]:
                            dve.wait_ge(rs_done, s + 3)
                            for i in range(NT):
                                last = v.tensor_scalar(xln[:, i, :], xln[:, i, :], mv[:, 0, i, 0:1],
                                                       rstd[:, 0, i:i + 1], ALU.subtract, ALU.mult)
                            last.then_inc(xln_done, 1)
                        if st.out and (h, t) == AT["ln2 stats"]:
                            ln_stats(x2[1 - st.par], 1, lambda: dve.wait_ge(gf_free, f_index(st, "O1") + 1),
                                     st2_done, mv2_done, ve2_done, s - 1)
                        if st.out and (h, t) == AT["ln2 norm"]:
                            dve.wait_ge(rs2_done, s)
                            if st.qk:
                                dve.wait_ge(ga_full, a_index(st, "K") + 1)
                            for i in range(NT):
                                last = v.tensor_scalar(yln[:, i, :], x2[1 - st.par][:, i, :], mv[:, 1, i, 0:1],
                                                       rstd[:, 1, i:i + 1], ALU.subtract, ALU.mult)
                            last.then_inc(yln_done, 1)
                    if not st.full and s == -1:
                        other_weights(h)

            def dve_a_task(st, task, n):
                kind = task[0]
                b, p = st.s + 1, 1 - st.par
                if kind == "K":
                    dve.wait_ge(cf_done, b + 1)
                    v.tensor_copy(cq[0:3 * DC, :], cf).then_inc(c_done, 1)
                    dve.wait_ge(c_done, 2 * b + 1)
                    mid = slice(DC, 2 * DC)
                    v.tensor_tensor(cq[mid, :], cf[mid, :], cq[mid, :], ALU.subtract).then_inc(c_done, 1)
                    dve.wait_ge(ga_free, n + 1)
                    wait(dve, st_full, (b - 1) * H * NT)
                    v.tensor_copy(KA[p][:, :], kf[:, :]).then_inc(k_done, 1)
                    dve.wait_ge(k_done, 2 * b + 1)
                    v.tensor_tensor(KB[p][0:W, :], kf[0:W, :], KA[p][0:W, :], ALU.subtract).then_inc(k_done, 1)
                elif kind == "S":
                    dve.wait_ge(ga_full, n + 1)
                    v.tensor_copy(const[p][:, :, :].rearrange("p t h -> p (t h)"), GA[:, 0:NT * H]).then_inc(ga_free, 1)
                elif kind == "Q":
                    h = int(task[1])
                    dve.wait_ge(qh_done, b * 2 * H + 2 * h + 1)
                    v.tensor_tensor(QA[W:2 * W, h, :], GA[W:2 * W, :], QA[W:2 * W, h, :],
                                    ALU.subtract).then_inc(ga_free, 1)

            def dve_f_task(st, task, n):
                kind, fbank = task[0], f_bank(st, n)
                if kind == "O":
                    i = int(task[1])
                    dve.wait_ge(gf_full, n + 1)
                    dve.wait_ge(xb_done, st.s)
                    two = x2[1 - st.par][:, 2 * i:2 * i + 2, :].rearrange("p t d -> p (t d)")
                    v.tensor_tensor(two, fbank[:, :], two, ALU.add).then_inc(gf_free, 1)
                elif kind == "T":
                    k = int(task[1])
                    dve.wait_ge(yh_done, (st.s - 1) * KD + k + 1)
                    v.tensor_tensor(yl[:, k, :], fbank[:, :], yh[:, k, :], ALU.subtract).then_inc(gf_free, 1)
                elif kind == "H":
                    f = int(task[1])
                    dve.wait_ge(gf_free, n + 1)
                    v.tensor_copy(hh[:, f, :], hidden(st, f)).then_inc(hh_done, 1)
                    if not st.sm:
                        dve.wait_ge(hh_done, (st.s - 2) * NF + f + 1)
                        v.tensor_tensor(hl[:, f, :], hidden(st, f), hh[:, f, :], ALU.subtract).then_inc(hl_done, 1)
                elif kind == "Y":
                    i = int(task[1])
                    dve.wait_ge(gf_full, n + 1)
                    if i == 0:
                        dve.wait_ge(x2b_done, st.s - 1)
                    if i == 0:
                        dve.wait_ge(hl_done, (st.s - 1) * NF)
                    if i >= 2:
                        dve.wait_ge(o_sent[i % 2], 8 * NT * (st.s - 2) + 32)
                    v.tensor_tensor(ob[:, i % 2, :], fbank[:, 0:D], x2[st.par][:, i, :], ALU.add).then_inc(gf_free, 1)

            steps(dve, step, q_weights)

        @block.tensor
        def _(pe):
            mm = nc.tensor.matmul
            tr = nc.tensor.transpose
            def q_weights():
                pe.wait_ge(cst, 7)
                pe.wait_ge(w_qk, 16 * N_QK)
                for w, to in ((wuq, tq), (wuk, tk)):
                    for h in range(H):
                        tr(to[:, h, :], w[:, h * DK:(h + 1) * DK], ident[0:DC, 0:DC])
                for j in range(2):
                    last = tr(tb[j], brow[:, j, :], ident[0:H, 0:H])
                last.then_inc(su_pe, 1)
                pe.wait_ge(su_dve, 2)
                pe.wait_ge(su_act, 1)
                for h in range(H):
                    last = mm(bank[2][0:KQ, h * (DC + 1):(h + 1) * (DC + 1)], LQ[:, h, :], RK[:, h, :],
                              start=True, stop=True)
                last.then_inc(su_pe, 1)

            def other_weights(h):
                if h == 2:
                    pe.wait_ge(w_o, 16 * N_O)
                    for i in range(H):
                        tr(tv[:, i, :], wuv[:, i * DK:(i + 1) * DK], ident[0:DC, 0:DC])
                    tr(tbv, brow[:, 2, :], ident[0:H, 0:H]).then_inc(su_pe, 1)
                if h == 3:
                    pe.wait_ge(su_act, 3)
                    mm(GF[:, 0:2], ones128, gsum, start=True, stop=True)
                    tr(GF[:, NF:2 * NF], b1row, ident[0:NF, 0:NF]).then_inc(su_pe, 1)
                    pe.wait_ge(su_act, 4)
                    for i in range(H):
                        r = (i % G) * DC
                        mm(ST[1][r:r + DC, 0:D], buv[:, i, :], wo[:, i, :], start=(i < G), stop=(i >= G))
                if h == 4:
                    for i in range(H):
                        r = (i % G) * DC
                        last = mm(ST[0][r:r + DC, (i // G) * D:(i // G + 1) * D], uvT[:, i, :], wo[:, i, :],
                                  start=True, stop=True)
                    last.then_inc(su_pe, 1)
                if h in (5, 6):
                    for i in range(4 * (h - 5), 4 * (h - 4)):
                        pe.wait_ge(su_dve, 14 if i < 4 else 16)
                        if i >= 2:
                            pe.wait_ge(su_act, max(5, 2 + i))
                        for j in range(4):
                            if i < 4:
                                src = w1n[:, (i % 2) * 4 + j, (i // 2) * P:(i // 2 + 1) * P]
                            else:
                                n = 2 * (i - 4) + j // 2
                                src = w2n[:, j % 2, n * P:(n + 1) * P]
                            last = tr(TURN[i % 4][:, j * P:(j + 1) * P], src, ident[:, :])
                        last.then_inc(su_pe, 1)
                if h == 5:
                    mm(L[:, 0:D], ones128, bsum, start=True, stop=True).then_inc(su_pe, 1)
                if h == 7:
                    pe.wait_ge(su_act, 13)
                    pe.wait_ge(su_dve, 17)

            def step(st):
                s = st.s
                for h in range(SLOTS):
                    for t in range(SEGS):
                        tok = slice(t * P, (t + 1) * P)
                        if st.sm:
                            n = s * H * NT + h * NT + t
                            if (h, t) == (0, 0):
                                pe.wait_ge(ga_free, a_index(before(st), "R0") + 1)
                            if (h, t) == (G, 0):
                                pe.wait_ge(ga_free, a_index(st, "R1") + 1)
                            wait(pe, e_done, n - 1)
                            mm(ST[t % 2][:, :], KA[st.par][:, tok], QA[:, h, :], start=True, stop=False)
                            mm(ST[t % 2][:, :], KB[st.par][0:W + G, tok], QB[:, h, :], start=False,
                               stop=True).then_inc(st_full, 1)
                        task = TASKS_A.get((h, t), "")
                        if task and st.has_a(task):
                            pe_a_task(st, task, a_index(st, task))
                        if (h >= 2 and st.qk) or (h < 2 and st.sm):
                            b, head, p = (s + 1, h - 2, 1 - st.par) if h >= 2 else (s, h + 6, st.par)
                            if t == 0:
                                src = st if h >= 2 else before(st)
                                pe.wait_ge(ga_free, a_index(src, f"Q{head}") + 1)
                            wait(pe, mx_done, b * H * NT + head * NT + t - 1)
                            mm(MX[t % 2][:, :], QA[:, head, tok], KA[p][:, :], start=True, stop=True).then_inc(mx_full, 1)
                        task = TASKS_F.get((h, t), "")
                        if task and st.has_f(task):
                            pe_f_task(st, task, f_index(st, task))
                        if t == 1 and ((h < G and st.out) or (h >= G and st.sm)):
                            b, gr, p = (s - 1, 1, 1 - st.par) if h < G else (s, 0, st.par)
                            i = h % G
                            if i == 0:
                                pe.wait_ge(e_done, (b * H + (gr + 1) * G) * NT)
                                wait(pe, un_done, b * NG + gr)
                            for j in range(G):
                                r = slice(j * DC, (j + 1) * DC)
                                last = mm(U[r, :], V[p][:, i, :], E[:, gr * G + j, i, :], start=(i == 0),
                                          stop=(i == NT - 1))
                            last.then_inc(pv_full, 1)
                        if ((h, t) == AT["sums 1"] and st.out) or ((h, t) == AT["sums 0"] and st.sm):
                            b, gr = (s - 1, 1) if (h, t) == AT["sums 1"] else (s, 0)
                            pe.wait_ge(es_done, (b * H + (gr + 1) * G) * 3)
                            wait(pe, rec_done, (b * NG + gr) * 4)
                            for j in range(G):
                                r = slice(j * DC, (j + 1) * DC)
                                last = mm(L[r, :], ones32[:, :], esum[:, j, :], start=True, stop=True)
                            last.then_inc(l_full, 1)
                    if not st.full and s == -1:
                        other_weights(h)

            def pe_a_task(st, task, n):
                kind = task[0]
                b, p = st.s + 1, 1 - st.par
                wait(pe, ga_free, n)
                tasks = [t for t in TASKS_A.values() if st.has_a(t)]
                came = tasks[tasks.index(task) - 1]
                if task == tasks[0]:
                    wait(pe, qh_done, b * 2 * H)
                elif came[0] == "Q":
                    pe.wait_ge(qh_done, b * 2 * H + 2 * int(came[1]) + 2)
                if kind == "X":
                    if task == "X0":
                        pe.wait_ge(xln_done, b + 1)
                    for t in range(NT):
                        last = tr(GA[:, t * P:(t + 1) * P], xln[:, t, int(task[1]) * P:(int(task[1]) + 1) * P],
                                  ident[:, :])
                elif kind == "K":
                    if not st.full and st.s == -1:
                        pe.wait_ge(w_x, 16 * N_X)
                    for k in range(KD):
                        last = mm(GA[0:W + DC, :], wk[:, k, :], xT[:, k, :], start=(k == 0), stop=(k == KD - 1))
                elif kind == "Q":
                    if task == "Q0":
                        pe.wait_ge(c_done, 2 * b + 2)
                        if not st.full and st.s == -1:
                            pe.wait_ge(su_dve, 10)
                    last = mm(GA[:, :], AQ[:, int(task[1]), :, :].rearrange("k a c -> k (a c)"), cq[0:KQ, :],
                              start=True, stop=True)
                elif kind == "S":
                    for t in range(NT):
                        last = mm(GA[:, t * H:(t + 1) * H], cq[0:KQ, t * P:(t + 1) * P], AC[:, :], start=True, stop=True)
                elif kind == "V":
                    for t in range(NT):
                        last = tr(GA[:, t * P:(t + 1) * P], kf[:, t * P:(t + 1) * P], ident[:, :])
                elif kind == "R":
                    gr = int(task[1])
                    pe.wait_ge(sh_done, (st.s if gr else b) * NG + gr + 1)
                    for t in range(NT):
                        last = mm(GA[0:W + G, t * P:(t + 1) * P], shift[:, t, :], identr[:, :], start=True, stop=True)
                last.then_inc(ga_full, 1)

            def pe_f_task(st, task, n):
                kind, fbank = task[0], f_bank(st, n)
                wait(pe, gf_free, f_freed(st, task, n))
                if not st.full and st.s == NB and task == "H0":
                    pe.wait_ge(ga_free, (NB - 1) * len(TASKS_A) + len(TASKS_A))
                i = int(task[1])
                if kind == "O":
                    if i == 0:
                        pe.wait_ge(un_done, st.s * NG)
                    for t in range(2):
                        q = slice((2 * i + t) * P, (2 * i + t + 1) * P)
                        for gr in range(NG):
                            last = mm(fbank[:, t * D:(t + 1) * D], un[:, gr, q], M[:, gr, :], start=(gr == 0),
                                      stop=(gr == NG - 1))
                elif kind == "T":
                    if i == 0:
                        pe.wait_ge(yln_done, st.s)
                    for t in range(NT):
                        last = tr(fbank[:, t * P:(t + 1) * P], yln[:, t, i * P:(i + 1) * P], ident[:, :])
                elif kind == "H":
                    f = slice(i * P, (i + 1) * P)
                    for k in range(KD):
                        mm(fbank[:, :], w1T[:, k, f], yh[:, k, :], start=(k == 0), stop=False)
                        last = mm(fbank[:, :], w1T[:, k, f], yl[:, k, :], start=False, stop=(k == KD - 1))
                elif kind == "Y":
                    q = slice(i * P, (i + 1) * P)
                    if i == 0:
                        pe.wait_ge(hl_done, (st.s - 1) * NF)
                    for f in range(NF):
                        mm(fbank[:, 0:D], hh[:, f, q], w2T[:, f, :], start=(f == 0), stop=False)
                        last = mm(fbank[:, 0:D], hl[:, f, q], w2T[:, f, :], start=False, stop=(f == NF - 1))
                last.then_inc(gf_full, 1)

            steps(pe, step, q_weights)


_INS = ["L0_attn_h_t", "L0_attn_W_DQ", "L0_attn_b_DQ", "L0_attn_W_UQ", "L0_attn_b_UQ", "L0_attn_W_DKV",
        "L0_attn_b_DKV", "L0_attn_W_UK", "L0_attn_b_UK", "L0_attn_W_UV", "L0_attn_b_UV", "L0_attn_W_QR",
        "L0_attn_b_QR", "L0_attn_W_KR", "L0_attn_b_KR", "L0_attn_W_O", "L0_attn_b_O", "L0_ffn_W1", "L0_ffn_b1",
        "L0_ffn_W2", "L0_ffn_b2"]


def kernel(**inputs):
    import numpy as _np
    import concourse.bacc as _bacc
    from concourse import mybir as _mybir
    from concourse.bass_utils import run_bass_kernel_spmd as _run

    nc = _bacc.Bacc("TRN2", target_bir_lowering=False, num_devices=1)
    arrays, args = {}, []
    for name in _INS:
        a = _np.ascontiguousarray(inputs[name])
        arrays[f"in_{name}"] = a
        args.append(nc.dram_tensor(f"in_{name}", a.shape, _mybir.dt.from_np(a.dtype), kind="ExternalInput").ap())
    shape = inputs["L0_attn_h_t"].shape
    args.append(nc.dram_tensor("out_0", shape, F32, kind="ExternalOutput").ap())
    layer_kernel(nc, *args)
    r = _run(nc, [arrays], core_ids=[0])
    return r.results[0]["out_0"]
```
